# Optimizing a Trainium2 kernel written in Bass

```python
import numpy as np
import jax
import jax.numpy as jnp

def _softmax(x, axis=-1):
    return jax.nn.softmax(x, axis=axis)

def _gelu(x):
    return jax.nn.gelu(x, approximate=True)

def _silu(x):
    return jax.nn.silu(x)

def _sigmoid(x):
    return jax.nn.sigmoid(x)

def _layernorm(x, axis=-1, eps=1e-05):
    m = jnp.mean(x, axis=axis, keepdims=True)
    v = jnp.var(x, axis=axis, keepdims=True)
    return (x - m) / jnp.sqrt(v + eps)

def _scatter_add(tgt, idx, src, axis=0):
    return tgt.at[idx].add(src)

def _segment_sum(src, seg, n):
    return jax.ops.segment_sum(src, seg, n)
kernel_name = 'mk_xattn_seq_d2_seqx_r8_5a7edd'

def setup_inputs(seed: int=0):
    np.random.seed(seed)
    _w = jnp.asarray

    def _rec_inputs():
        import jax
        import jax.numpy as jnp
        _rk = jax.random.key(seed)
        x = 7.22e-05 + 1 * jax.random.normal(jax.random.fold_in(_rk, 1), (8, 128, 256), jnp.float32)
        _lenS = 128 - jax.random.randint(jax.random.fold_in(_rk, 7), (8,), 0, max(1, 128 // 4) + 1, jnp.int32)
        _lenS2 = 128 - jax.random.randint(jax.random.fold_in(_rk, 8), (8,), 0, max(1, 128 // 4) + 1, jnp.int32)
        _ctx_2048P = jax.random.normal(jax.random.fold_in(_rk, 11), (8, 16, 256), jnp.float32)
        _ctx_2048c = jax.random.dirichlet(jax.random.fold_in(_rk, 511), 0.3 * jnp.ones((16,), jnp.float32), (8, 128))
        _ctx_2048t = jnp.einsum('bsk,bkd->bsd', _ctx_2048c, _ctx_2048P)
        _ctx_2048t = _ctx_2048t * jax.lax.rsqrt(jnp.mean(jnp.square(_ctx_2048t)) + 1e-12) * 0.953939
        ctx_2048 = 4.13588e-05 + 0.999923 * (_ctx_2048t + 0.3 * jax.random.normal(jax.random.fold_in(_rk, 611), (8, 128, 256), jnp.float32))
        _validS = jnp.arange(128)[None, :] < _lenS[:, None]
        _validS2 = jnp.arange(128)[None, :] < _lenS2[:, None]
        _causal = jnp.tril(jnp.ones((128, 128), dtype=bool))
        mask_Bx1xSxS2_ff0 = jnp.where(jnp.ones((8, 1, 128, 128), dtype=bool), 0.0, -1000000000.0).astype(jnp.float32)
        mask_BxS2_bf1 = jnp.ones((8, 128), dtype=bool)
        return (x, ctx_2048, mask_Bx1xSxS2_ff0, mask_BxS2_bf1)
    x, ctx_2048, mask_Bx1xSxS2_ff0, mask_BxS2_bf1 = _rec_inputs()

    def _L0_xattn_setup():
        import jax, jax.numpy as jnp
        import numpy as np
        H = 256
        NH = 32
        KVH = 8
        HD = H // NH
        GROUPS = NH // KVH
        EPS = 1e-06
        B, L, S = (4, 128, 128)

        def _gqa_forward(hidden_state, encoder_hidden_state, encoder_attention_mask, Wq, bq, Wk, bk, Wv, bv, Wo, bo, gamma, beta):
            b, l, _ = hidden_state.shape
            s = encoder_hidden_state.shape[1]
            q = hidden_state @ Wq + bq
            k = encoder_hidden_state @ Wk + bk
            v = encoder_hidden_state @ Wv + bv
            q = q.reshape(b, l, KVH, GROUPS, HD).transpose(0, 2, 3, 1, 4)
            k = k.reshape(b, s, KVH, HD).transpose(0, 2, 1, 3)
            v = v.reshape(b, s, KVH, HD).transpose(0, 2, 1, 3)
            scale = 1.0 / jnp.sqrt(jnp.asarray(HD, q.dtype))
            scores = jnp.einsum('bkgld,bksd->bkgls', q, k) * scale
            scores = scores + encoder_attention_mask[:, :, None, :, :]
            attn = jax.nn.softmax(scores, axis=-1)
            out = jnp.einsum('bkgls,bksd->bkgld', attn, v)
            out = out.transpose(0, 3, 1, 2, 4).reshape(b, l, H)
            out = out @ Wo + bo
            x = out + hidden_state
            mu = jnp.mean(x, axis=-1, keepdims=True)
            var = jnp.var(x, axis=-1, keepdims=True)
            return (x - mu) * jax.lax.rsqrt(var + EPS) * gamma + beta
        key = jax.random.key(seed)
        ks = jax.random.split(key, 12)
        sd = 0.02
        return {'hidden_state': jax.random.normal(ks[0], (B, L, H), jnp.float32), 'encoder_hidden_state': jax.random.normal(ks[1], (B, S, H), jnp.float32), 'encoder_attention_mask': jnp.zeros((B, 1, L, S), jnp.float32), 'Wq': jax.random.normal(ks[2], (H, H), jnp.float32) * sd, 'bq': jnp.zeros((H,), jnp.float32), 'Wk': jax.random.normal(ks[3], (H, KVH * HD), jnp.float32) * sd, 'bk': jnp.zeros((KVH * HD,), jnp.float32), 'Wv': jax.random.normal(ks[4], (H, KVH * HD), jnp.float32) * sd, 'bv': jnp.zeros((KVH * HD,), jnp.float32), 'Wo': jax.random.normal(ks[5], (H, H), jnp.float32) * sd, 'bo': jnp.zeros((H,), jnp.float32), 'gamma': jnp.ones((H,), jnp.float32), 'beta': jnp.zeros((H,), jnp.float32)}
    _L0_xattn_all = _L0_xattn_setup()
    _L0_xattn_in = {k: v for k, v in _L0_xattn_all.items() if k in ('Wq', 'bq', 'Wk', 'bk', 'Wv', 'bv', 'Wo', 'bo', 'gamma', 'beta')}
    del _L0_xattn_all

    def _L1_xattn_setup():
        import jax, jax.numpy as jnp
        import numpy as np
        D = 256
        H = 16
        HD = D // H
        INNER = 4 * D
        EPS = 1e-05

        def layer_norm(x, w, b):
            mu = jnp.mean(x, axis=-1, keepdims=True)
            var = jnp.mean(jnp.square(x - mu), axis=-1, keepdims=True)
            return (x - mu) * jax.lax.rsqrt(var + EPS) * w + b
        key = jax.random.key(seed)
        ks = jax.random.split(key, 12)
        B, LQ, LK = (4, 128, 256)
        std = 0.02
        inp = {'hidden_states': jax.random.normal(ks[0], (B, LQ, D), jnp.float32), 'encoder_hidden_states': jax.random.normal(ks[1], (B, LK, D), jnp.float32), 'encoder_attention_mask': jnp.ones((B, LK), dtype=bool), 'ln1_w': jnp.ones((D,), jnp.float32), 'ln1_b': jnp.zeros((D,), jnp.float32), 'q_w': jax.random.normal(ks[2], (D, D), jnp.float32) * std, 'q_b': jnp.zeros((D,), jnp.float32), 'k_w': jax.random.normal(ks[3], (D, D), jnp.float32) * std, 'k_b': jnp.zeros((D,), jnp.float32), 'v_w': jax.random.normal(ks[4], (D, D), jnp.float32) * std, 'v_b': jnp.zeros((D,), jnp.float32), 'cproj_w': jax.random.normal(ks[5], (D, D), jnp.float32) * std, 'cproj_b': jnp.zeros((D,), jnp.float32), 'ln2_w': jnp.ones((D,), jnp.float32), 'ln2_b': jnp.zeros((D,), jnp.float32), 'fc_w': jax.random.normal(ks[6], (D, INNER), jnp.float32) * std, 'fc_b': jnp.zeros((INNER,), jnp.float32), 'proj_w': jax.random.normal(ks[7], (INNER, D), jnp.float32) * std, 'proj_b': jnp.zeros((D,), jnp.float32)}
        return inp
    _L1_xattn_all = _L1_xattn_setup()
    _L1_xattn_in = {k: v for k, v in _L1_xattn_all.items() if k in ('ln1_w', 'ln1_b', 'q_w', 'q_b', 'k_w', 'k_b', 'v_w', 'v_b', 'cproj_w', 'cproj_b', 'ln2_w', 'ln2_b', 'fc_w', 'fc_b', 'proj_w', 'proj_b')}
    del _L1_xattn_all
    return {'x': x, 'ctx_2048': ctx_2048, 'mask_Bx1xSxS2_ff0': mask_Bx1xSxS2_ff0, 'mask_BxS2_bf1': mask_BxS2_bf1, 'L0_xattn_Wq': _L0_xattn_in['Wq'], 'L0_xattn_bq': _L0_xattn_in['bq'], 'L0_xattn_Wk': _L0_xattn_in['Wk'], 'L0_xattn_bk': _L0_xattn_in['bk'], 'L0_xattn_Wv': _L0_xattn_in['Wv'], 'L0_xattn_bv': _L0_xattn_in['bv'], 'L0_xattn_Wo': _L0_xattn_in['Wo'], 'L0_xattn_bo': _L0_xattn_in['bo'], 'L0_xattn_gamma': _L0_xattn_in['gamma'], 'L0_xattn_beta': _L0_xattn_in['beta'], 'L1_xattn_ln1_w': _L1_xattn_in['ln1_w'], 'L1_xattn_ln1_b': _L1_xattn_in['ln1_b'], 'L1_xattn_q_w': _L1_xattn_in['q_w'], 'L1_xattn_q_b': _L1_xattn_in['q_b'], 'L1_xattn_k_w': _L1_xattn_in['k_w'], 'L1_xattn_k_b': _L1_xattn_in['k_b'], 'L1_xattn_v_w': _L1_xattn_in['v_w'], 'L1_xattn_v_b': _L1_xattn_in['v_b'], 'L1_xattn_cproj_w': _L1_xattn_in['cproj_w'], 'L1_xattn_cproj_b': _L1_xattn_in['cproj_b'], 'L1_xattn_ln2_w': _L1_xattn_in['ln2_w'], 'L1_xattn_ln2_b': _L1_xattn_in['ln2_b'], 'L1_xattn_fc_w': _L1_xattn_in['fc_w'], 'L1_xattn_fc_b': _L1_xattn_in['fc_b'], 'L1_xattn_proj_w': _L1_xattn_in['proj_w'], 'L1_xattn_proj_b': _L1_xattn_in['proj_b']}

def reference(x, ctx_2048, mask_Bx1xSxS2_ff0, mask_BxS2_bf1, L0_xattn_Wq, L0_xattn_bq, L0_xattn_Wk, L0_xattn_bk, L0_xattn_Wv, L0_xattn_bv, L0_xattn_Wo, L0_xattn_bo, L0_xattn_gamma, L0_xattn_beta, L1_xattn_ln1_w, L1_xattn_ln1_b, L1_xattn_q_w, L1_xattn_q_b, L1_xattn_k_w, L1_xattn_k_b, L1_xattn_v_w, L1_xattn_v_b, L1_xattn_cproj_w, L1_xattn_cproj_b, L1_xattn_ln2_w, L1_xattn_ln2_b, L1_xattn_fc_w, L1_xattn_fc_b, L1_xattn_proj_w, L1_xattn_proj_b):
    import jax
    import jax.numpy as jnp

    def _L0_xattn_ref(hidden_state, encoder_hidden_state, encoder_attention_mask, Wq, bq, Wk, bk, Wv, bv, Wo, bo, gamma, beta):
        import jax, jax.numpy as jnp
        import numpy as np
        H = 256
        NH = 32
        KVH = 8
        HD = H // NH
        GROUPS = NH // KVH
        EPS = 1e-06
        B, L, S = (4, 128, 128)

        def _gqa_forward(hidden_state, encoder_hidden_state, encoder_attention_mask, Wq, bq, Wk, bk, Wv, bv, Wo, bo, gamma, beta):
            b, l, _ = hidden_state.shape
            s = encoder_hidden_state.shape[1]
            q = hidden_state @ Wq + bq
            k = encoder_hidden_state @ Wk + bk
            v = encoder_hidden_state @ Wv + bv
            q = q.reshape(b, l, KVH, GROUPS, HD).transpose(0, 2, 3, 1, 4)
            k = k.reshape(b, s, KVH, HD).transpose(0, 2, 1, 3)
            v = v.reshape(b, s, KVH, HD).transpose(0, 2, 1, 3)
            scale = 1.0 / jnp.sqrt(jnp.asarray(HD, q.dtype))
            scores = jnp.einsum('bkgld,bksd->bkgls', q, k) * scale
            scores = scores + encoder_attention_mask[:, :, None, :, :]
            attn = jax.nn.softmax(scores, axis=-1)
            out = jnp.einsum('bkgls,bksd->bkgld', attn, v)
            out = out.transpose(0, 3, 1, 2, 4).reshape(b, l, H)
            out = out @ Wo + bo
            x = out + hidden_state
            mu = jnp.mean(x, axis=-1, keepdims=True)
            var = jnp.var(x, axis=-1, keepdims=True)
            return (x - mu) * jax.lax.rsqrt(var + EPS) * gamma + beta
        return _gqa_forward(hidden_state, encoder_hidden_state, encoder_attention_mask, Wq, bq, Wk, bk, Wv, bv, Wo, bo, gamma, beta)

    def _L1_xattn_ref(hidden_states, encoder_hidden_states, encoder_attention_mask, ln1_w, ln1_b, q_w, q_b, k_w, k_b, v_w, v_b, cproj_w, cproj_b, ln2_w, ln2_b, fc_w, fc_b, proj_w, proj_b):
        import jax, jax.numpy as jnp
        import numpy as np
        D = 256
        H = 16
        HD = D // H
        INNER = 4 * D
        EPS = 1e-05

        def layer_norm(x, w, b):
            mu = jnp.mean(x, axis=-1, keepdims=True)
            var = jnp.mean(jnp.square(x - mu), axis=-1, keepdims=True)
            return (x - mu) * jax.lax.rsqrt(var + EPS) * w + b
        B, LQ, _ = hidden_states.shape
        LK = encoder_hidden_states.shape[1]
        residual = hidden_states
        x = layer_norm(hidden_states, ln1_w, ln1_b)
        q = (x @ q_w + q_b).reshape(B, LQ, H, HD).transpose(0, 2, 1, 3)
        k = (encoder_hidden_states @ k_w + k_b).reshape(B, LK, H, HD).transpose(0, 2, 1, 3)
        v = (encoder_hidden_states @ v_w + v_b).reshape(B, LK, H, HD).transpose(0, 2, 1, 3)
        scale = 1.0 / np.sqrt(HD).astype(np.float32)
        scores = jnp.einsum('bhqd,bhkd->bhqk', q, k) * scale
        mask = encoder_attention_mask[:, None, None, :]
        mask_value = jnp.finfo(scores.dtype).min
        scores = jnp.where(mask, scores, mask_value)
        attn = jax.nn.softmax(scores, axis=-1)
        out = jnp.einsum('bhqk,bhkd->bhqd', attn, v)
        out = out.transpose(0, 2, 1, 3).reshape(B, LQ, D)
        out = out @ cproj_w + cproj_b
        hidden = out + residual
        residual = hidden
        y = layer_norm(hidden, ln2_w, ln2_b)
        y = jax.nn.gelu(y @ fc_w + fc_b, approximate=True)
        y = y @ proj_w + proj_b
        return residual + y
    x = _L0_xattn_ref(x, ctx_2048, mask_Bx1xSxS2_ff0, L0_xattn_Wq, L0_xattn_bq, L0_xattn_Wk, L0_xattn_bk, L0_xattn_Wv, L0_xattn_bv, L0_xattn_Wo, L0_xattn_bo, L0_xattn_gamma, L0_xattn_beta)
    x = _L1_xattn_ref(x, ctx_2048, mask_BxS2_bf1, L1_xattn_ln1_w, L1_xattn_ln1_b, L1_xattn_q_w, L1_xattn_q_b, L1_xattn_k_w, L1_xattn_k_b, L1_xattn_v_w, L1_xattn_v_b, L1_xattn_cproj_w, L1_xattn_cproj_b, L1_xattn_ln2_w, L1_xattn_ln2_b, L1_xattn_fc_w, L1_xattn_fc_b, L1_xattn_proj_w, L1_xattn_proj_b)
    return x

_drawn_inputs = setup_inputs


def setup_inputs(seed=0):
    import zlib

    import numpy as np

    out = dict(_drawn_inputs(seed))
    spreads = {'L0_xattn_bq': (0.0, 0.8),
     'L0_xattn_bk': (0.0, 0.8),
     'L0_xattn_bv': (0.0, 0.1),
     'L0_xattn_bo': (0.0, 0.1),
     'L0_xattn_gamma': (1.0, 0.2),
     'L0_xattn_beta': (0.0, 0.1),
     'L1_xattn_ln1_w': (1.0, 0.6),
     'L1_xattn_ln1_b': (0.0, 0.8),
     'L1_xattn_q_b': (0.0, 0.8),
     'L1_xattn_k_b': (0.0, 0.8),
     'L1_xattn_v_b': (0.0, 0.277),
     'L1_xattn_cproj_b': (0.0, 0.1),
     'L1_xattn_ln2_w': (1.0, 0.6),
     'L1_xattn_ln2_b': (0.0, 0.8),
     'L1_xattn_fc_b': (0.0, 0.1),
     'L1_xattn_proj_b': (0.0, 0.1)}
    factors = {'L0_xattn_Wq': 8.0, 'L0_xattn_Wk': 8.0, 'L1_xattn_q_w': 8.0, 'L1_xattn_k_w': 8.0}
    for name, (base, spread) in spreads.items():
        noise = np.random.default_rng([zlib.crc32(name.encode()), seed]).standard_normal(out[name].shape)
        drawn = base * np.exp(spread * noise) if base else spread * noise
        out[name] = jnp.asarray(drawn.astype(out[name].dtype))
    for name, factor in factors.items():
        out[name] = (out[name] * factor).astype(out[name].dtype)
    return out
```

```python
import concourse.bass as bass
from concourse import mybir
from contextlib import ExitStack

F32 = mybir.dt.float32
BF16 = mybir.dt.bfloat16
I32 = mybir.dt.int32
ALU = mybir.AluOpType
ACT = mybir.ActivationFunctionType
AX = mybir.AxisListType

NB = 8
P = 128
D = 256
C = D // P
H0, KV0, D0 = 32, 8, 8
H1, D1 = 16, 16
G0 = H0 // KV0
FF = 4 * D
FC = FF // P
R0 = 6 * D0
R1 = 6 * D1
M0R = R0 + 3
M1R = R1 + 1
M1E = M1R + 3
S0 = float(D0) ** -0.5
S1 = float(D1) ** -0.5
EPS0, EPS1 = 1e-6, 1e-5
MASKED = 2.0 ** 100
LOWEST = -3.0e38
TH = 4
T0 = H0 // TH
T1 = H1 // TH
NT = T0 + T1
W = 32
NP = 4

COL = dict(q0=0, k0=2, k1=3, q1=5, w1=7, b1=9, w2=11, b2=13, fc=15)
NCOL = 15 + FC
VEC, _at = {}, 0
for _name, _n in (("v0", KV0 * D0), ("v1", D), ("bo", D), ("gamma", D), ("beta", D), ("cp", D), ("pb", D)):
    VEC[_name] = (_at, _at + _n)
    _at += _n
NVEC = _at


def build(nc, x, xT, cT, mask, kmask, eye, cols, vecs, wqk, wv, wo, wk1, wq1, wv1, wcp, wfc, wpj, out):
    with ExitStack() as ctx:
        def sb(name, shape, dt=F32):
            return ctx.enter_context(nc.sbuf_tensor(name, shape, dt))

        def ps(name, shape):
            return ctx.enter_context(nc.psum_tensor(name, shape, F32))

        def sem(name):
            return ctx.enter_context(nc.semaphore(name))

        ident = sb("ident", [P, P])
        col = sb("col", [P, NCOL])
        vec = sb("vec", [P, NVEC])
        w_qk = sb("w_qk", [P, C, D + P])
        w_v0 = sb("w_v0", [P, C, KV0 * D0])
        w_o = sb("w_o", [P, C, D])
        w_k1 = sb("w_k1", [P, C, D])
        w_q1 = sb("w_q1", [P, C, D])
        w_v1 = sb("w_v1", [P, C, D])
        w_cp = sb("w_cp", [P, C, D])
        w_fc = sb("w_fc", [P, C, FF])
        w_pj = sb("w_pj", [P, FC, D])
        maskq = sb("maskq", [P, NB, P])
        mcur = sb("mcur", [P, 2, P])
        mcl = [sb(f"mcl{i}", [P, P]) for i in range(2)]
        kmu = sb("kmu", [P, 2, P], mybir.dt.uint8)
        kmr = sb("kmr", [NB, P], mybir.dt.uint8)
        kbias = sb("kbias", [NB, P], BF16)
        absm = sb("absm", [P, 1])
        flag = sb("flag", [1, 1])
        half = sb("half", [P, 1])
        xs = sb("xs", [P, 2, D])
        xTs = sb("xTs", [P, 2, C, P])
        cTs = sb("cTs", [P, 2, C, P])
        xb = sb("xb", [P, 2, D])
        qk32 = sb("qk32", [P, 3, 2 * P])
        qkr = sb("qkr", [P, 3, 2 * P])
        qkp = sb("qkp", [P, 3, 3, 2 * P], BF16)
        q32 = sb("q32", [P, 2 * P])
        q1r = sb("q1r", [P, 2 * P])
        q1p = sb("q1p", [P, 3, 2 * P], BF16)
        QS0 = [sb(f"QS0_{i}", [P, H0, P], BF16) for i in range(2)]
        KS0 = [sb(f"KS0_{i}", [P, KV0, P], BF16) for i in range(2)]
        KS1 = [sb(f"KS1_{i}", [P, H1, P], BF16) for i in range(2)]
        QS1 = sb("QS1", [P, H1, P], BF16)
        V0 = [sb(f"V0_{i}", [P, KV0, W]) for i in range(2)]
        V1 = [sb(f"V1_{i}", [P, H1, W]) for i in range(2)]
        ot0 = sb("ot0", [P, 2, TH * P])
        ot1 = sb("ot1", [P, TH * P])
        negm = sb("negm", [P, P])
        sbias = sb("sbias", [P, 4])
        kmf = sb("kmf", [NB, P])
        mr = sb("mr", [H0 + H1, P])
        mp = sb("mp", [H0 + H1, 3, P], BF16)
        prob = [sb(f"prob{i}", [P, TH, P]) for i in range(NP)]
        rd0 = sb("rd0", [P, 2, H0 // 2, 1])
        rd1 = sb("rd1", [P, H1, 1])
        at0 = sb("at0", [P, H0, D0])
        at1 = sb("at1", [P, H1, D1])
        at0T = sb("at0T", [P, C, P])
        at1T = sb("at1T", [P, C, P])
        h0 = sb("h0", [P, D])
        h1 = sb("h1", [P, D])
        hb = sb("hb", [P, 2, D])
        st0 = sb("st0", [P, 6])
        st1 = sb("st1", [P, 6])
        st2 = sb("st2", [P, 6])
        mv0 = sb("mv0", [P, 2])
        mv1 = sb("mv1", [P, 2])
        mv2 = sb("mv2", [P, 2])
        ve0 = sb("ve0", [P, 1])
        ve1 = sb("ve1", [P, 1])
        ve2 = sb("ve2", [P, 1])
        rs0 = sb("rs0", [P, 1])
        rs1 = sb("rs1", [P, 1])
        rs2 = sb("rs2", [P, 1])
        xg = sb("xg", [P, D])
        x1 = sb("x1", [P, D])
        x1b = sb("x1b", [P, 2, D])
        xn = sb("xn", [P, D])
        yn = sb("yn", [P, D])
        xnT = sb("xnT", [P, C, P])
        yT = sb("yT", [P, C, P])
        hT = sb("hT", [P, FC, P])
        ob = sb("ob", [P, 2, D])

        A = [ps(f"A{i}", [P, 512]) for i in range(2)]
        B = [ps(f"B{i}", [P, 512]) for i in range(2)]
        M = [ps(f"M{i}", [P, 512]) for i in range(2)]
        V = [ps(f"V{i}", [P, 512]) for i in range(2)]

        def scratch(name, shape):
            return nc.dram_tensor(name, shape, BF16, kind="Internal").ap()

        dq0 = [scratch(f"dq0_{i}", (3, D0, H0, P)) for i in range(2)]
        dk0 = [scratch(f"dk0_{i}", (3, D0, KV0, P)) for i in range(2)]
        dk1 = [scratch(f"dk1_{i}", (3, D1, H1, P)) for i in range(2)]
        dq1 = scratch("dq1", (3, D1, H1, P))
        dkb = scratch("dkb", (NB, P))

        names = """set_io set_mask set_km set_w set_kbd set_dve set_absT set_pool sp_go mk_in mk_ok km_in
                   x_in xT_in cT_in xb_ok
                   qk_ps v_ps k1_ps qk_ev k1_ev v_ev sp_hi sp_r sp_mid sp_lo
                   dq0_w dk0_w dk1_w k1_m
                   negT m_hi m_r m_mid m_lo m0_in m1_in
                   ot0_ok ot1_ok ott0_ps ott1_ps rd0_ok rd1_ok at0_ok at1_ok
                   at0T_ps at1T_ps at0T_ok at1T_ok o0_ps o1_ps
                   h0_ok st0_ok mv0_ok ve0_ok rs0_ok xg_ok x1_ok x1b_ok st1_ok mv1_ok ve1_ok rs1_ok xn_ok
                   h1_ok hb_ok st2_ok mv2_ok ve2_ok rs2_ok yn_ok
                   xnT_ps xnT_ok yT_ps yT_ok q1_ps q1_ev q1_hi q1_r q1_mid q1_lo dq1_w
                   h_ps hT_ok y_ps out_ok st_even st_odd""".split()
        S = {n: sem("s_" + n) for n in names}
        q0_in, k0_in, k1_in, q1_in = (sem("s_" + n) for n in ("q0_in", "k0_in", "k1_in", "q1_in"))
        a_ps = [sem(f"s_a_ps{k}") for k in range(NT)]
        a_max = [sem(f"s_a_max{k}") for k in range(NT)]
        b_ps = [sem(f"s_b_ps{k}") for k in range(NT)]
        b_exp = [sem(f"s_b_exp{k}") for k in range(NT)]
        pv_ok = [sem(f"s_pv{k}") for k in range(NT)]

        def steps(eng, step):
            def peeled(s):
                step(s, s // 2, s % 2, 0 <= s < NB, 1 <= s <= NB, 2 <= s <= NB + 1, s < NB - 1)

            for s in (-1, 0, 1):
                peeled(s)
            with eng.Fori(1, (NB - 2) // 2) as i:
                step(2 * i, i, 0, True, True, True, True)
                step(2 * i + 1, i, 1, True, True, True, True)
            for s in range(NB - 2, NB + 2):
                peeled(s)

        def vslice(name):
            a, b = VEC[name]
            return vec[:, a:b]

        def stack(eng, done, src, dst, d, query):
            for part, reps, row in ((0, 3, 0), (1, 2, 3), (2, 1, 5)):
                if query:
                    eng.dma_start(dst[row * d:(row + reps) * d].rearrange("p h t -> p (h t)"),
                                  src[0:reps].rearrange("j d h t -> (j d) (h t)")).then_inc(done, 16)
                else:
                    one = src[part:part + 1].rearrange("j d h t -> j d (h t)")
                    eng.dma_start(dst[row * d:(row + reps) * d].rearrange("p h t -> p (h t)"),
                                  one.broadcast_to([reps, d, one.shape[2]])).then_inc(done, 16)

        def of(dram, b):
            return dram[b] if isinstance(b, int) else dram[bass.ds(b, 1)].squeeze(0)

        block = ctx.enter_context(nc.Block())

        @block.sync
        def _(sp):
            sp.sem_inc(S["st_even"], 16)
            sp.sem_inc(S["st_odd"], 16)
            for dst, src in ((xTs[:, 0], xT[0]), (w_qk[:], wqk), (col[:], cols), (cTs[:, 0], cT[0]), (w_v0[:], wv),
                             (vec[:], vecs.partition_broadcast(P)), (ident[:], eye), (xs[:, 0], x[0])):
                sp.dma_start(dst, src).then_inc(S["set_io"], 16)
            sp.dma_start(kmr[:], kmask).then_inc(S["set_km"], 16)
            sp.dma_start(maskq[:], mask.rearrange("b q k -> q b k")).then_inc(S["set_mask"], 16)
            sp.dma_start(mcur[:, 0], mask[0]).then_inc(S["mk_in"], 16)
            sp.dma_start(kmu[:, 0], kmask[0].partition_broadcast(P)).then_inc(S["km_in"], 16)
            for dst, src in ((w_k1, wk1), (w_v1, wv1), (w_o, wo), (w_q1, wq1), (w_cp, wcp), (w_fc, wfc), (w_pj, wpj)):
                sp.dma_start(dst[:], src).then_inc(S["set_w"], 16)
            sp.wait_ge(S["set_pool"], 5)
            sp.dma_start(dkb, kbias[:]).then_inc(S["set_kbd"], 16)
            sp.wait_ge(S["set_kbd"], 16)

            def step(s, pair, slot, l0, l1, l2, pre):
                other = 1 - slot
                if l0 and pre:
                    if not (isinstance(s, int) and s == 0):
                        sp.wait_ge(S["xb_ok"], s)
                        sp.sem_inc(S["sp_go"], 1)
                        sp.wait_ge(S["v_ps"], s + 1)
                        sp.wait_ge(S["k1_ps"], s)
                        sp.wait_ge(S["mk_ok"], s)
                        sp.wait_ge(S["k1_ev"], s)
                        sp.sem_inc(S["sp_go"], 1)
                    sp.dma_start(xTs[:, other], of(xT, s + 1)).then_inc(S["xT_in"], 16)
                    sp.dma_start(cTs[:, other], of(cT, s + 1)).then_inc(S["cT_in"], 16)
                    sp.dma_start(xs[:, other], of(x, s + 1)).then_inc(S["x_in"], 16)
                    sp.dma_start(mcur[:, other], of(mask, s + 1)).then_inc(S["mk_in"], 16)
                    sp.dma_start(kmu[:, other], of(kmask, s + 1).partition_broadcast(P)).then_inc(S["km_in"], 16)
                if l0 or l1:
                    sp.wait_ge(S["m_lo"], s + 1)
                    if l0:
                        for j in range(3):
                            sp.dma_start(QS0[slot][R0 + j:R0 + j + 1], mp[0:H0, j]).then_inc(S["m0_in"], 16)
                    if l1:
                        for j in range(3):
                            sp.dma_start(QS1[M1R + j:M1R + j + 1], mp[H0:H0 + H1, j]).then_inc(S["m1_in"], 16)
                if l0 or pre:
                    sp.wait_ge(S["sp_lo"], s + 2)
                if pre:
                    sp.dma_start(dq0[other].rearrange("j (c d) h t -> (d h) (j c) t", c=C),
                                 qkp[:, 0].rearrange("p j (c t) -> p (j c) t", c=C)).then_inc(S["dq0_w"], 16)
                    sp.dma_start(dk0[other].rearrange("j d h t -> (d h) j t"), qkp[0:KV0 * D0, 1, :, 0:P]).then_inc(S["dk0_w"], 16)
                if l0:
                    sp.dma_start(dk1[slot].rearrange("j (c d) h t -> (d h) (j c) t", c=C),
                                 qkp[:, 2].rearrange("p j (c t) -> p (j c) t", c=C)).then_inc(S["dk1_w"], 16)
                if pre:
                    sp.wait_ge(S["dq0_w"], 16 * (s + 2))
                    stack(sp, q0_in, dq0[other], QS0[other], D0, True)
                    sp.wait_ge(S["dk0_w"], 16 * (s + 2))
                    stack(sp, k0_in, dk0[other], KS0[other], D0, False)
                if l0:
                    sp.wait_ge(S["dk1_w"], 16 * (s + 1))
                    stack(sp, k1_in, dk1[slot], KS1[slot], D1, False)
                    sp.wait_ge(S["set_kbd"], 16)
                    sp.dma_start(KS1[slot][R1:M1R], of(dkb, s).unsqueeze(0).unsqueeze(0).broadcast_to([1, H1, P])).then_inc(S["k1_m"], 16)
                if l2:
                    sp.wait_ge(S["set_kbd"], 16)
                    sp.wait_ge(S["out_ok"], s - 1)
                    sp.dma_start(of(out, s - 2), ob[:, slot]).then_inc(S["st_odd" if slot else "st_even"], 16)
                if l0:
                    sp.wait_ge(S["q1_lo"], s + 1)
                    sp.dma_start(dq1.rearrange("j (c d) h t -> (d h) (j c) t", c=C),
                                 q1p[:].rearrange("p j (c t) -> p (j c) t", c=C)).then_inc(S["dq1_w"], 16)
                    sp.wait_ge(S["dq1_w"], 16 * (s + 1))
                    if l1:
                        sp.wait_ge(b_ps[NT - 1], s)
                    stack(sp, q1_in, dq1, QS1, D1, True)

            steps(sp, step)
            sp.wait_ge(S["st_even"], 16 * (NB // 2 + 1))
            sp.wait_ge(S["st_odd"], 16 * (NB // 2 + 1))

        @block.tensor
        def _(pe):
            mm = nc.tensor.matmul
            pe.wait_ge(S["set_io"], 16 * 8)
            pe.wait_ge(S["set_dve"], 3)
            nc.tensor.transpose(V[0][0:1, 0:P], absm[:], ident[:]).then_inc(S["set_absT"], 1)
            pe.wait_ge(S["set_dve"], 4)
            any_mask = pe.value_load(flag[:].bitcast(I32), min_val=0, max_val=2 ** 31 - 1)

            def tile_a(s, slot, k, masked, bank_of):
                if bank_of is not None:
                    pe.wait_ge(a_max[bank_of], s + 1 if bank_of < T0 else s)
                for j in range(TH):
                    if k < T0:
                        last = mm(A[k % 2][:, j * P:(j + 1) * P], QS0[slot][0:R0, k * G0 + j], KS0[slot][0:R0, k],
                                  start=j == 0, stop=not masked, skip_group_check=True)
                    else:
                        h = (k - T0) * TH + j
                        last = mm(A[k % 2][:, j * P:(j + 1) * P], QS1[0:M1R, h], KS1[1 - slot][0:M1R, h],
                                  start=j == 0, stop=True, skip_group_check=True)
                if masked and k < T0:
                    last = mm(A[k % 2][:].rearrange("p (g k) -> p g k", g=G0), ident[:],
                              mcl[slot][:].unsqueeze(1).broadcast_to([P, G0, P]), start=False, stop=True, skip_group_check=True)
                last.then_inc(a_ps[k], 1)

            def pass_a(s, slot, tiles, masked, extras):
                for n, k in enumerate(tiles):
                    if k == T0:
                        pe.wait_ge(q1_in, 48 * s)
                        pe.wait_ge(k1_in, 48 * s)
                        pe.wait_ge(S["k1_m"], 16 * s)
                    tile_a(s, slot, k, masked, tiles[n - 2] if n >= 2 else None)
                    for f in extras.get(k, ()):
                        f()

            def tile_b(s, slot, k, masked, bank_of):
                if bank_of is not None:
                    pe.wait_ge(b_exp[bank_of], s + 1 if bank_of < T0 else s)
                if k < T0:
                    last = mm(B[k % 2][:], KS0[slot][0:M0R, k], QS0[slot][0:M0R, k * G0:(k + 1) * G0],
                              start=True, stop=not masked, skip_group_check=True)
                    if masked:
                        for g in range(G0):
                            last = mm(B[k % 2][:, g * P:(g + 1) * P], mcl[slot][:], ident[:], start=False, stop=True,
                                      skip_group_check=True)
                else:
                    for j in range(TH):
                        h = (k - T0) * TH + j
                        last = mm(B[k % 2][:, j * P:(j + 1) * P], KS1[1 - slot][0:M1E, h], QS1[0:M1E, h],
                                  start=j == 0, stop=True, skip_group_check=True)
                last.then_inc(b_ps[k], 1)

            def tile_pv(s, slot, k):
                pe.wait_ge(b_exp[k], s + 1 if k < T0 else s)
                if k < T0:
                    q = k % TH * W
                    last = mm(V[k // TH][q:q + W, :], V0[slot][:, k], prob[k % NP][:].rearrange("p h t -> p (h t)"),
                              start=True, stop=True, skip_group_check=True)
                else:
                    for j in range(TH):
                        h = (k - T0) * TH + j
                        last = mm(V[0][j * W:(j + 1) * W, (k - T0) * P:(k - T0 + 1) * P], V1[1 - slot][:, h], prob[k % NP][:, j],
                                  start=True, stop=True, skip_group_check=True)
                last.then_inc(pv_ok[k], 1)

            def pass_b(s, slot, tiles, masked, extras):
                for n, k in enumerate(tiles[:2]):
                    tile_b(s, slot, k, masked, None)
                for n, k in enumerate(tiles):
                    if n + 2 < len(tiles):
                        if tiles[n + 2] == T0:
                            pe.wait_ge(S["m1_in"], 48 * s)
                        tile_b(s, slot, tiles[n + 2], masked, k)
                    if k == T0 and tiles[0] < T0:
                        pe.wait_ge(S["ot0_ok"], 2 * s + 1)
                    tile_pv(s, slot, k)
                    for f in extras.get(k, ()):
                        f()

            def flip(dst, src, done):
                for c in range(C):
                    last = nc.tensor.transpose(dst[:, c * P:(c + 1) * P], src[:, c * P:(c + 1) * P], ident[:])
                last.then_inc(done, 1)

            def tokens_out(dst, lhs, w, start_first=True):
                chunks = w.shape[1]
                for c in range(chunks):
                    last = mm(dst, lhs[:, c], w[:, c], start=c == 0 and start_first, stop=c == chunks - 1, skip_group_check=True)
                return last

            def dims_out(dst, w, rhs, m):
                for c in range(C):
                    last = mm(dst, w[:, c, m * P:(m + 1) * P], rhs[:, c], start=m == 0 and c == 0, stop=c == C - 1, skip_group_check=True)
                return last

            def turn(dst, src, done):
                for t in range(TH):
                    last = nc.tensor.transpose(dst[:, t * P:(t + 1) * P], src[:, t * P:(t + 1) * P], ident[:])
                last.then_inc(done, 1)

            def step(s, pair, slot, l0, l1, l2, pre):
                other = 1 - slot
                first = isinstance(s, int) and s <= 0
                tiles = list(range(T0)) * l0 + list(range(T0, NT)) * l1

                def mlp_up(m):
                    for c in range(C):
                        last = mm(B[m // TH][:, m % TH * P:(m % TH + 1) * P], w_fc[:, c, m * P:(m + 1) * P], yT[:, c],
                                  start=m % TH == 0 and c == 0, stop=c == C - 1, skip_group_check=True)
                    if m % TH == TH - 1:
                        last.then_inc(S["h_ps"], 1)

                def mlp_down(m):
                    if m == 0:
                        if l0:
                            pe.wait_ge(S["v_ev"], s + 2)
                        else:
                            pe.wait_ge(S["h1_ok"], s - 1)
                    last = mm(M[1][:, 0:D], hT[:, m], w_pj[:, m], start=m == 0, stop=m == FC - 1, skip_group_check=True)
                    if m == FC - 1:
                        last.then_inc(S["y_ps"], 1)

                def spread(f):
                    extras = {}
                    n = min(len(tiles), FC)
                    for m in range(FC if l2 else 0):
                        extras.setdefault(tiles[m * n // FC], []).append(lambda m=m: f(m))
                    return extras

                if l2:
                    pe.wait_ge(S["yT_ok"], s - 1)
                if l0:
                    pe.wait_ge(q0_in, 48 * (s + 1))
                    pe.wait_ge(k0_in, 48 * (s + 1))
                    pe.wait_ge(S["mk_ok"], s + 1)
                    with pe.If(any_mask > 0):
                        pass_a(s, slot, tiles, True, spread(mlp_up))
                    with pe.Else():
                        pass_a(s, slot, tiles, False, spread(mlp_up))
                    pe.nop()
                elif l1:
                    pass_a(s, slot, tiles, False, spread(mlp_up))
                elif l2:
                    for m in range(FC):
                        mlp_up(m)
                if l0 or l1:
                    if l0:
                        pe.wait_ge(a_max[T0 - 1], s + 1)
                    if l1:
                        pe.wait_ge(a_max[NT - 1], s)
                    nc.tensor.transpose(V[0][:, 0:P], negm[:], ident[:]).then_inc(S["negT"], 1)

                if pre:
                    if l0:
                        pe.wait_ge(S["xT_in"], 16 * (s + 1))
                        pe.wait_ge(S["cT_in"], 16 * (s + 1))
                        if first:
                            pe.wait_ge(S["qk_ev"], s + 1)
                    for m in range(C):
                        dims_out(M[0][:, m * P:(m + 1) * P], w_qk, xTs[:, other], m)
                    for c in range(C):
                        last = mm(M[0][:, D:D + P], w_qk[:, c, D:D + P], cTs[:, other, c], start=False, stop=c == C - 1,
                                  skip_group_check=True)
                    last.then_inc(S["qk_ps"], 1)
                if l0:
                    if first:
                        pe.wait_ge(S["v_ev"], s + 1)
                    else:
                        pe.wait_ge(S["q1_ev"], s)
                        if not (isinstance(s, int) and s == 1):
                            pe.wait_ge(S["h1_ok"], s - 1)
                if pre:
                    last = tokens_out(M[1][:, 0:KV0 * D0], cTs[:, other], w_v0)
                if l0:
                    if first:
                        pe.wait_ge(S["set_w"], 16 * 7)
                    last = tokens_out(M[1][:, P:P + D], cTs[:, slot], w_v1, not pre)
                if l0 or pre:
                    last.then_inc(S["v_ps"], 1)
                if l0:
                    if pre:
                        pe.wait_ge(S["qk_ev"], s + 2)
                    for m in range(C):
                        last = dims_out(M[0][:, m * P:(m + 1) * P], w_k1, cTs[:, slot], m)
                    last.then_inc(S["k1_ps"], 1)

                def turn0(a):
                    def go():
                        pe.wait_ge(S["ot0_ok"], 2 * s + 1 + a)
                        turn(A[a], ot0[:, a], S["ott0_ps"])
                    return go

                def at0_flip():
                    pe.wait_ge(S["at0_ok"], 2 * s + 2)
                    pe.wait_ge(S["k1_ev"], s + 1)
                    flip(M[0], at0[:].rearrange("p h d -> p (h d)"), S["at0T_ps"])

                extras = spread(mlp_down) if tiles else {}
                tail0 = [turn0(0), turn0(1), at0_flip] if l0 else []
                if l0 and l1:
                    for k, f in zip((NT - 3, NT - 2, NT - 1), tail0):
                        extras.setdefault(k, []).append(f)
                    tail0 = []
                if l2:
                    pe.wait_ge(S["hT_ok"], s - 1)
                if l0:
                    pe.wait_ge(S["m0_in"], 48 * (s + 1))
                    with pe.If(any_mask > 0):
                        pass_b(s, slot, tiles, True, extras)
                    with pe.Else():
                        pass_b(s, slot, tiles, False, extras)
                    pe.nop()
                elif l1:
                    pe.wait_ge(S["m1_in"], 48 * s)
                    pass_b(s, slot, tiles, False, extras)
                elif l2:
                    for m in range(FC):
                        mlp_down(m)
                for f in tail0:
                    f()

                if l0:
                    pe.wait_ge(S["at0T_ok"], s + 1)
                    if l2:
                        pe.wait_ge(S["out_ok"], s - 1)
                    else:
                        pe.wait_ge(S["v_ev"], s + 2)
                    tokens_out(M[1][:, 0:D], at0T, w_o).then_inc(S["o0_ps"], 1)
                if l1:
                    pe.wait_ge(S["ot1_ok"], s)
                    turn(A[0], ot1[:], S["ott1_ps"])
                if l0:
                    pe.wait_ge(S["xn_ok"], s + 1)
                    flip(M[0], xn[:], S["xnT_ps"])
                    pe.wait_ge(S["xnT_ok"], s + 1)
                    pe.wait_ge(S["h0_ok"], s + 1)
                    for m in range(C):
                        last = dims_out(M[1][:, m * P:(m + 1) * P], w_q1, xnT, m)
                    last.then_inc(S["q1_ps"], 1)
                if l1:
                    pe.wait_ge(S["at1_ok"], s)
                    flip(M[0], at1[:].rearrange("p h d -> p (h d)"), S["at1T_ps"])
                    pe.wait_ge(S["at1T_ok"], s)
                    if l0:
                        pe.wait_ge(S["q1_ev"], s + 1)
                    else:
                        pe.wait_ge(S["out_ok"], s - 1)
                    tokens_out(M[1][:, 0:D], at1T, w_cp).then_inc(S["o1_ps"], 1)
                    pe.wait_ge(S["yn_ok"], s)
                    flip(M[0], yn[:], S["yT_ps"])

            steps(pe, step)

        @block.vector
        def _(dve):
            v = nc.vector
            v.memset(qk32[:], 0.0)
            v.memset(negm[:], 0.0)
            for i in range(2):
                v.memset(KS0[i][32:2 * 32], 1.0)
                v.memset(KS1[i][R1:P], 1.0)
            v.memset(QS1[R1:P], 1.0)
            for i in range(2):
                v.memset(V0[i][:], 0.0)
                v.memset(V1[i][:], 0.0).then_inc(S["set_dve"], 1)
            dve.wait_ge(S["set_dve"], 2)
            for i in range(2):
                v.memset(V0[i][:, :, D0:D0 + 1], 1.0)
                v.memset(V1[i][:, :, D1:D1 + 1], 1.0)
            dve.wait_ge(S["set_mask"], 16)
            v.tensor_reduce(absm[:], maskq[:].rearrange("p b k -> p (b k)"), AX.X, ALU.max, apply_absolute_value=True)\
                .then_inc(S["set_dve"], 1)
            dve.wait_ge(S["set_absT"], 1)
            v.tensor_reduce(flag[:], V[0][0:1, 0:P], AX.X, ALU.max).then_inc(S["set_dve"], 1)

            def norm_stats(x_, wait, n, st, mv, ve, eps, tags):
                dve.wait_ge(*wait)
                v.bn_stats(st[:], x_).then_inc(S[tags[0]], 1)
                dve.wait_ge(S["set_dve"], 2)
                dve.wait_ge(S[tags[0]], n)
                v.bn_aggr(mv[:], st[:]).then_inc(S[tags[1]], 1)
                dve.wait_ge(S[tags[1]], n)
                v.tensor_scalar(ve[:], mv[:, 1:2], eps, None, ALU.add).then_inc(S[tags[2]], 1)

            def step(s, pair, slot, l0, l1, l2, pre):
                other = 1 - slot
                for k in range(NT):
                    if (k < T0 and l0) or (k >= T0 and l1):
                        dve.wait_ge(a_ps[k], s + 1 if k < T0 else s)
                        v.tensor_reduce(negm[:, k * TH:(k + 1) * TH], A[k % 2][:].rearrange("p (g k) -> p g k", g=TH),
                                        AX.X, ALU.max, negate=True).then_inc(a_max[k], 1)
                if l0 or l1:
                    H = H0 + H1
                    dve.wait_ge(S["negT"], s + 1)
                    v.tensor_copy(mp[:, 0], V[0][0:H, 0:P]).then_inc(S["m_hi"], 1)
                    dve.wait_ge(S["m_hi"], s + 1)
                    v.tensor_tensor(mr[:], V[0][0:H, 0:P], mp[:, 0], ALU.subtract).then_inc(S["m_r"], 1)
                    dve.wait_ge(S["m_r"], s + 1)
                    v.tensor_copy(mp[:, 1], mr[:]).then_inc(S["m_mid"], 1)
                    dve.wait_ge(S["m_mid"], s + 1)
                    v.tensor_tensor(mp[:, 2], mr[:], mp[:, 1], ALU.subtract).then_inc(S["m_lo"], 1)
                if l0 or pre:
                    dve.wait_ge(S["v_ps"], s + 2)
                    if not (l0 or l1):
                        dve.wait_ge(S["set_io"], 16 * 8)
                if pre:
                    last = v.tensor_tensor(V0[other][:, :, 0:D0], M[1][:, 0:KV0 * D0].rearrange("p (h d) -> p h d", d=D0),
                                           vslice("v0").rearrange("p (h d) -> p h d", d=D0), ALU.add)
                if l0:
                    last = v.tensor_tensor(V1[slot][:, :, 0:D1], M[1][:, P:P + D].rearrange("p (h d) -> p h d", d=D1),
                                           vslice("v1").rearrange("p (h d) -> p h d", d=D1), ALU.add)
                if l0 or pre:
                    last.then_inc(S["v_ev"], 1)
                if l0:
                    dve.wait_ge(S["k1_ps"], s + 1)
                    dve.wait_ge(S["km_in"], 16 * (s + 1))
                    dve.wait_ge(S["sp_lo"], s + 1)
                    for c in range(C):
                        last = v.scalar_tensor_tensor(qk32[:, 2, c * P:(c + 1) * P], M[0][:, c * P:(c + 1) * P],
                                                      col[:, COL["k1"] + c:COL["k1"] + c + 1], kmu[:, slot], ALU.add, ALU.mult)
                    last.then_inc(S["k1_ev"], 1)
                if pre:
                    dve.wait_ge(S["mk_in"], 16 * (s + 2))
                    v.tensor_scalar(mcl[other][:], mcur[:, other], LOWEST, None, ALU.max).then_inc(S["mk_ok"], 1)
                if l2:
                    dve.wait_ge(S["y_ps"], s - 1)
                    dve.wait_ge(S["hb_ok"], s - 1)
                    dve.wait_ge(S["st_odd" if slot else "st_even"], 16 * pair)
                    v.tensor_tensor(ob[:, slot], M[1][:, 0:D], hb[:, slot], ALU.add).then_inc(S["out_ok"], 1)
                if l0:
                    for a in range(2):
                        pv = A[a][:].rearrange("p (g j w) -> p j g w", j=TH, w=W)
                        r = rd0[:, a].rearrange("p (j g) o -> p j g o", g=G0)
                        dve.wait_ge(S["ott0_ps"], 2 * s + 1 + a)
                        v.reciprocal(r, pv[:, :, :, D0:D0 + 1]).then_inc(S["rd0_ok"], 1)
                        dve.wait_ge(S["rd0_ok"], 2 * s + 1 + a)
                        v.tensor_tensor(at0[:, a * H0 // 2:(a + 1) * H0 // 2].rearrange("p (j g) d -> p j g d", g=G0),
                                        pv[:, :, :, 0:D0], r.broadcast_to([P, TH, G0, D0]), ALU.mult).then_inc(S["at0_ok"], 1)
                    dve.wait_ge(S["o0_ps"], s + 1)
                    dve.wait_ge(S["xb_ok"], s + 1)
                    v.tensor_tensor(h0[:], M[1][:, 0:D], xb[:, slot], ALU.add).then_inc(S["h0_ok"], 1)
                    norm_stats(h0[:], (S["h0_ok"], s + 1), s + 1, st0, mv0, ve0, EPS0, ("st0_ok", "mv0_ok", "ve0_ok"))
                    v.scalar_tensor_tensor(xg[:], h0[:], mv0[:, 0:1], vslice("gamma"), ALU.subtract, ALU.mult).then_inc(S["xg_ok"], 1)
                pv1 = A[0][:].rearrange("p (h w) -> p h w", w=W)
                if l1:
                    dve.wait_ge(S["ott1_ps"], s)
                    v.reciprocal(rd1[:], pv1[:, :, D1:D1 + 1]).then_inc(S["rd1_ok"], 1)
                if l0:
                    dve.wait_ge(S["rs0_ok"], s + 1)
                    dve.wait_ge(S["xg_ok"], s + 1)
                    v.scalar_tensor_tensor(x1[:], xg[:], rs0[:], vslice("beta"), ALU.mult, ALU.add).then_inc(S["x1_ok"], 1)
                    norm_stats(x1[:], (S["x1_ok"], s + 1), s + 1, st1, mv1, ve1, EPS1, ("st1_ok", "mv1_ok", "ve1_ok"))
                if l1:
                    dve.wait_ge(S["rd1_ok"], s)
                    v.tensor_tensor(at1[:], pv1[:, :, 0:D1], rd1[:].broadcast_to([P, H1, D1]), ALU.mult).then_inc(S["at1_ok"], 1)
                if l0:
                    dve.wait_ge(S["rs1_ok"], s + 1)
                    v.tensor_scalar(xn[:], x1[:], mv1[:, 0:1], rs1[:], ALU.subtract, ALU.mult).then_inc(S["xn_ok"], 1)
                    dve.wait_ge(S["q1_hi"], s + 1)
                    v.tensor_tensor(q1r[:], q32[:], q1p[:, 0], ALU.subtract).then_inc(S["q1_r"], 1)
                    dve.wait_ge(S["q1_mid"], s + 1)
                    v.tensor_tensor(q1p[:, 2], q1r[:], q1p[:, 1], ALU.subtract).then_inc(S["q1_lo"], 1)
                if l1:
                    dve.wait_ge(S["o1_ps"], s)
                    dve.wait_ge(S["x1b_ok"], s)
                    v.tensor_tensor(h1[:], M[1][:, 0:D], x1b[:, other], ALU.add).then_inc(S["h1_ok"], 1)
                    norm_stats(h1[:], (S["h1_ok"], s), s, st2, mv2, ve2, EPS1, ("st2_ok", "mv2_ok", "ve2_ok"))
                    dve.wait_ge(S["rs2_ok"], s)
                    v.tensor_scalar(yn[:], h1[:], mv2[:, 0:1], rs2[:], ALU.subtract, ALU.mult).then_inc(S["yn_ok"], 1)

            steps(dve, step)

        @block.scalar
        def _(act):
            a = nc.scalar.activation
            act.wait_ge(S["set_io"], 16 * 8)
            act.wait_ge(S["set_pool"], 3)

            def step(s, pair, slot, l0, l1, l2, pre):
                if l2:
                    for m in range(FC):
                        if m % TH == 0:
                            act.wait_ge(S["h_ps"], 2 * s - 3 + m // TH)
                        last = a(hT[:, m], B[m // TH][:, (m % TH) * P:(m % TH + 1) * P], ACT.Gelu_apprx_tanh,
                                 bias=col[:, COL["fc"] + m:COL["fc"] + m + 1])
                    last.then_inc(S["hT_ok"], 1)
                if pre:
                    act.wait_ge(S["qk_ps"], s + 2)
                    if l0:
                        act.wait_ge(S["sp_lo"], s + 1)
                    else:
                        act.wait_ge(S["set_dve"], 2)
                    for c in range(C):
                        a(qk32[:, 0, c * P:(c + 1) * P], M[0][:, c * P:(c + 1) * P], ACT.Identity, bias=sbias[:, c:c + 1], scale=S0)
                    a(qk32[:, 1, 0:P], M[0][:, D:D + P], ACT.Identity, bias=col[:, COL["k0"]:COL["k0"] + 1]).then_inc(S["qk_ev"], 1)
                    act.wait_ge(S["qk_ev"], s + 2)
                if l0 or pre:
                    if l0:
                        act.wait_ge(S["k1_ev"], s + 1)
                        act.wait_ge(S["dq0_w"], 16 * (s + 1))
                        act.wait_ge(S["dk0_w"], 16 * (s + 1))
                        if not (isinstance(s, int) and s == 0):
                            act.wait_ge(S["dk1_w"], 16 * s)
                    a(qkp[:, :, 0], qk32[:], ACT.Copy).then_inc(S["sp_hi"], 1)

                def tile(k):
                    act.wait_ge(b_ps[k], s + 1 if k < T0 else s)
                    if k >= NP and (l0 or k >= T0 + NP):
                        act.wait_ge(pv_ok[k - NP], s + 1 if k - NP < T0 else s)
                    a(prob[k % NP][:].rearrange("p h t -> p (h t)"), B[k % 2][:], ACT.Exp).then_inc(b_exp[k], 1)

                def sums0(half_):
                    act.wait_ge(pv_ok[(half_ + 1) * TH - 1], s + 1)
                    a(ot0[:, half_], V[half_][:], ACT.Copy).then_inc(S["ot0_ok"], 1)

                if l0:
                    tile(0)
                    tile(1)
                if l0 or pre:
                    act.wait_ge(S["sp_r"], s + 2)
                    a(qkp[:, :, 1], qkr[:], ACT.Copy).then_inc(S["sp_mid"], 1)
                for k in range(2 if l0 else T0, NT if l1 else T0):
                    if k == TH + 2:
                        sums0(0)
                    if k == 2 * TH + 2 and l0:
                        sums0(1)
                    tile(k)
                if l0:
                    if not l1:
                        sums0(1)
                    act.wait_ge(S["at0T_ps"], s + 1)
                    a(at0T[:].rearrange("p c t -> p (c t)"), M[0][:, 0:D], ACT.Copy).then_inc(S["at0T_ok"], 1)
                if l1:
                    act.wait_ge(pv_ok[NT - 1], s)
                    a(ot1[:], V[0][:], ACT.Copy).then_inc(S["ot1_ok"], 1)
                if l0:
                    act.wait_ge(S["xnT_ps"], s + 1)
                    for c in range(C):
                        last = a(xnT[:, c], M[0][:, c * P:(c + 1) * P], ACT.Identity, bias=col[:, COL["b1"] + c:COL["b1"] + c + 1],
                                 scale=col[:, COL["w1"] + c:COL["w1"] + c + 1])
                    last.then_inc(S["xnT_ok"], 1)
                    act.wait_ge(S["q1_ps"], s + 1)
                    for c in range(C):
                        last = a(q32[:, c * P:(c + 1) * P], M[1][:, c * P:(c + 1) * P], ACT.Identity, bias=sbias[:, 2 + c:3 + c], scale=S1)
                    last.then_inc(S["q1_ev"], 1)
                    act.wait_ge(S["q1_ev"], s + 1)
                    if l1:
                        act.wait_ge(S["dq1_w"], 16 * s)
                    a(q1p[:, 0], q32[:], ACT.Copy).then_inc(S["q1_hi"], 1)
                    act.wait_ge(S["q1_r"], s + 1)
                    a(q1p[:, 1], q1r[:], ACT.Copy).then_inc(S["q1_mid"], 1)
                if l1:
                    act.wait_ge(S["at1T_ps"], s)
                    a(at1T[:].rearrange("p c t -> p (c t)"), M[0][:, 0:D], ACT.Copy).then_inc(S["at1T_ok"], 1)
                    act.wait_ge(S["yT_ps"], s)
                    for c in range(C):
                        last = a(yT[:, c], M[0][:, c * P:(c + 1) * P], ACT.Identity, bias=col[:, COL["b2"] + c:COL["b2"] + c + 1],
                                 scale=col[:, COL["w2"] + c:COL["w2"] + c + 1])
                    last.then_inc(S["yT_ok"], 1)

            steps(act, step)

        @block.gpsimd
        def _(pool):
            g = nc.gpsimd
            g.memset(half[:], -0.5).then_inc(S["set_pool"], 1)
            pool.wait_ge(S["set_pool"], 1)
            pool.wait_ge(S["set_io"], 16 * 8)
            g.tensor_scalar(sbias[:, 0:2], col[:, COL["q0"]:COL["q0"] + 2], S0, None, ALU.mult).then_inc(S["set_pool"], 1)
            pool.wait_ge(S["set_pool"], 2)
            g.tensor_scalar(sbias[:, 2:4], col[:, COL["q1"]:COL["q1"] + 2], S1, None, ALU.mult).then_inc(S["set_pool"], 1)
            pool.wait_ge(S["set_km"], 16)
            g.tensor_copy(kmf[:], kmr[:]).then_inc(S["set_pool"], 1)
            pool.wait_ge(S["set_pool"], 4)
            g.tensor_scalar(kbias[:], kmf[:], 1.0, MASKED, ALU.subtract, ALU.mult).then_inc(S["set_pool"], 1)

            def inverse_root(ve, rs, n, t_in, t_out):
                pool.wait_ge(S[t_in], n)
                g.tensor_tensor(rs[:], ve[:], half[:], ALU.pow).then_inc(S[t_out], 1)

            def step(s, pair, slot, l0, l1, l2, pre):
                other = 1 - slot
                if pre:
                    if l0:
                        pool.wait_ge(S["x_in"], 16 * (s + 1))
                    g.tensor_tensor(xb[:, other], xs[:, other], vslice("bo"), ALU.add).then_inc(S["xb_ok"], 1)
                if l0 or pre:
                    pool.wait_ge(S["sp_hi"], s + 2)
                    g.tensor_tensor(qkr[:], qk32[:], qkp[:, :, 0], ALU.subtract).then_inc(S["sp_r"], 1)
                    pool.wait_ge(S["sp_mid"], s + 2)
                    g.tensor_tensor(qkp[:, :, 2], qkr[:], qkp[:, :, 1], ALU.subtract).then_inc(S["sp_lo"], 1)
                if l0:
                    inverse_root(ve0, rs0, s + 1, "ve0_ok", "rs0_ok")
                    inverse_root(ve1, rs1, s + 1, "ve1_ok", "rs1_ok")
                    g.tensor_tensor(x1b[:, slot], x1[:], vslice("cp"), ALU.add).then_inc(S["x1b_ok"], 1)
                if l1:
                    inverse_root(ve2, rs2, s, "ve2_ok", "rs2_ok")
                    g.tensor_tensor(hb[:, other], h1[:], vslice("pb"), ALU.add).then_inc(S["hb_ok"], 1)

            steps(pool, step)


_OUT = (NB, P, D)


def kernel(**inputs):
    import numpy as np
    import concourse.bacc as bacc
    from concourse import mybir as mb
    from concourse.bass_utils import run_bass_kernel_spmd as run

    g = {k: np.asarray(v) for k, v in inputs.items()}

    def rows(w):
        return w.reshape(-1, P, w.shape[1]).transpose(1, 0, 2)

    def heads_inner(w, h, d):
        return w.reshape(w.shape[:-1] + (h, d)).swapaxes(-1, -2).reshape(w.shape)

    def column(b):
        return b.reshape(-1, P).T

    L0, L1 = "L0_xattn_", "L1_xattn_"
    wk0 = heads_inner(g[L0 + "Wk"], KV0, D0)
    bk0 = heads_inner(g[L0 + "bk"], KV0, D0)
    turned = lambda t: t.transpose(0, 2, 1).reshape(NB, C, P, P).transpose(0, 2, 1, 3)
    data = dict(
        x=g["x"], xT=turned(g["x"]), cT=turned(g["ctx_2048"]),
        mask=g["mask_Bx1xSxS2_ff0"].reshape(NB, P, P), kmask=g["mask_BxS2_bf1"],
        eye=np.eye(P, dtype=np.float32),
        cols=np.concatenate([
            column(heads_inner(g[L0 + "bq"], H0, D0)), column(np.concatenate([bk0, bk0])),
            column(heads_inner(g[L1 + "k_b"], H1, D1)), column(heads_inner(g[L1 + "q_b"], H1, D1)),
            column(g[L1 + "ln1_w"]), column(g[L1 + "ln1_b"]), column(g[L1 + "ln2_w"]), column(g[L1 + "ln2_b"]),
            column(g[L1 + "fc_b"])], axis=1),
        vecs=np.concatenate([g[L0 + "bv"], g[L1 + "v_b"], g[L0 + "bo"], g[L0 + "gamma"], g[L0 + "beta"],
                             g[L1 + "cproj_b"], g[L1 + "proj_b"]]),
        wqk=rows(np.concatenate([heads_inner(g[L0 + "Wq"], H0, D0), wk0, wk0], axis=1)),
        wv=rows(g[L0 + "Wv"]), wo=rows(g[L0 + "Wo"]),
        wk1=rows(heads_inner(g[L1 + "k_w"], H1, D1)), wq1=rows(heads_inner(g[L1 + "q_w"], H1, D1)),
        wv1=rows(g[L1 + "v_w"]), wcp=rows(g[L1 + "cproj_w"]), wfc=rows(g[L1 + "fc_w"]), wpj=rows(g[L1 + "proj_w"]),
    )
    nc = bacc.Bacc("TRN2", target_bir_lowering=False, num_devices=1)
    arrays, args = {}, {}
    for name, a in data.items():
        a = np.ascontiguousarray(a)
        arrays["in_" + name] = a
        args[name] = nc.dram_tensor("in_" + name, a.shape, mb.dt.from_np(a.dtype), kind="ExternalInput").ap()
    args["out"] = nc.dram_tensor("out_0", _OUT, F32, kind="ExternalOutput").ap()
    build(nc, **args)
    r = run(nc, [arrays], core_ids=[0])
    return r.results[0]["out_0"]
```

```python
import concourse.bass as bass
from concourse import mybir
from contextlib import ExitStack

F32 = mybir.dt.float32
BF16 = mybir.dt.bfloat16
I32 = mybir.dt.int32
ALU = mybir.AluOpType
ACT = mybir.ActivationFunctionType
AX = mybir.AxisListType

NB = 8
P = 128
D = 256
C = D // P
H0, KV0, D0 = 32, 8, 8
H1, D1 = 16, 16
G0 = H0 // KV0
FF = 4 * D
FC = FF // P
R0 = 6 * D0
R1 = 6 * D1
M0R = R0 + 3
M1R = R1 + 1
M1E = M1R + 3
S0 = float(D0) ** -0.5
S1 = float(D1) ** -0.5
EPS0, EPS1 = 1e-6, 1e-5
MASKED = 2.0 ** 100
LOWEST = -3.0e38
TH = 4
T0 = H0 // TH
T1 = H1 // TH
NT = T0 + T1
W = 32
NP = 4

COL = dict(q0=0, k0=2, k1=3, q1=5, w1=7, b1=9, w2=11, b2=13, fc=15)
NCOL = 15 + FC
VEC, _at = {}, 0
for _name, _n in (("v0", KV0 * D0), ("v1", D), ("bo", D), ("gamma", D), ("beta", D), ("cp", D), ("pb", D)):
    VEC[_name] = (_at, _at + _n)
    _at += _n
NVEC = _at


def build(nc, x, xT, cT, mask, kmask, eye, cols, vecs, wqk, wv, wo, wk1, wq1, wv1, wcp, wfc, wpj, out):
    with ExitStack() as ctx:
        def sb(name, shape, dt=F32):
            return ctx.enter_context(nc.sbuf_tensor(name, shape, dt))

        def ps(name, shape):
            return ctx.enter_context(nc.psum_tensor(name, shape, F32))

        def sem(name):
            return ctx.enter_context(nc.semaphore(name))

        ident = sb("ident", [P, P])
        col = sb("col", [P, NCOL])
        vec = sb("vec", [P, NVEC])
        w_qk = sb("w_qk", [P, C, D + P])
        w_v0 = sb("w_v0", [P, C, KV0 * D0])
        w_o = sb("w_o", [P, C, D])
        w_k1 = sb("w_k1", [P, C, D])
        w_q1 = sb("w_q1", [P, C, D])
        w_v1 = sb("w_v1", [P, C, D])
        w_cp = sb("w_cp", [P, C, D])
        w_fc = sb("w_fc", [P, C, FF])
        w_pj = sb("w_pj", [P, FC, D])
        maskq = sb("maskq", [P, NB, P])
        mcur = sb("mcur", [P, 2, P])
        mcl = [sb(f"mcl{i}", [P, P]) for i in range(2)]
        kmu = sb("kmu", [P, 2, P], mybir.dt.uint8)
        kmr = sb("kmr", [NB, P], mybir.dt.uint8)
        kbias = sb("kbias", [NB, P], BF16)
        absm = sb("absm", [P, 1])
        flag = sb("flag", [1, 1])
        half = sb("half", [P, 1])
        xs = sb("xs", [P, 2, D])
        xTs = sb("xTs", [P, 2, C, P])
        cTs = sb("cTs", [P, 2, C, P])
        xb = sb("xb", [P, 2, D])
        qk32 = sb("qk32", [P, 2, 2 * P])
        qkr = sb("qkr", [P, 2, 2 * P])
        qkp = sb("qkp", [P, 2, 3, 2 * P], BF16)
        k32 = sb("k32", [P, 2 * P])
        k1r = sb("k1r", [P, 2 * P])
        k1p = sb("k1p", [P, 3, 2 * P], BF16)
        q32 = sb("q32", [P, 2 * P])
        q1r = sb("q1r", [P, 2 * P])
        q1p = sb("q1p", [P, 3, 2 * P], BF16)
        QS0 = [sb(f"QS0_{i}", [P, H0, P], BF16) for i in range(2)]
        KS0 = [sb(f"KS0_{i}", [P, KV0, P], BF16) for i in range(2)]
        KS1 = [sb(f"KS1_{i}", [P, H1, P], BF16) for i in range(2)]
        QS1 = sb("QS1", [P, H1, P], BF16)
        V0 = [sb(f"V0_{i}", [P, KV0, W]) for i in range(2)]
        V1 = [sb(f"V1_{i}", [P, H1, W]) for i in range(2)]
        ot0 = sb("ot0", [P, 2, TH * P])
        ot1 = sb("ot1", [P, TH * P])
        negm0 = sb("negm0", [P, P])
        negm1 = sb("negm1", [P, P])
        sbias = sb("sbias", [P, 4])
        kmf = sb("kmf", [NB, P])
        m0r = sb("m0r", [H0, P])
        m0p = sb("m0p", [H0, 3, P], BF16)
        m1r = sb("m1r", [H1, P])
        m1p = sb("m1p", [H1, 3, P], BF16)
        prob = [sb(f"prob{i}", [P, TH, P]) for i in range(NP)]
        rd0 = sb("rd0", [P, 2, H0 // 2, 1])
        rd1 = sb("rd1", [P, H1, 1])
        at0 = sb("at0", [P, H0, D0])
        at1 = sb("at1", [P, H1, D1])
        at0T = sb("at0T", [P, C, P])
        at1T = sb("at1T", [P, C, P])
        h0 = sb("h0", [P, D])
        h1 = sb("h1", [P, D])
        hb = sb("hb", [P, D])
        st0 = sb("st0", [P, 6])
        st1 = sb("st1", [P, 6])
        st2 = sb("st2", [P, 6])
        mv0 = sb("mv0", [P, 2])
        mv1 = sb("mv1", [P, 2])
        mv2 = sb("mv2", [P, 2])
        ve0 = sb("ve0", [P, 1])
        ve1 = sb("ve1", [P, 1])
        ve2 = sb("ve2", [P, 1])
        rs0 = sb("rs0", [P, 1])
        rs1 = sb("rs1", [P, 1])
        rs2 = sb("rs2", [P, 1])
        xg = sb("xg", [P, D])
        x1 = sb("x1", [P, D])
        x1b = sb("x1b", [P, 2, D])
        xn = sb("xn", [P, D])
        yn = sb("yn", [P, D])
        xnT = sb("xnT", [P, C, P])
        yT = sb("yT", [P, C, P])
        hT = sb("hT", [P, FC, P])
        ob = sb("ob", [P, 2, D])

        A = [ps(f"A{i}", [P, 512]) for i in range(2)]
        B = [ps(f"B{i}", [P, 512]) for i in range(2)]
        M = [ps(f"M{i}", [P, 512]) for i in range(2)]
        V = [ps(f"V{i}", [P, 512]) for i in range(2)]

        def scratch(name, shape):
            return nc.dram_tensor(name, shape, BF16, kind="Internal").ap()

        dq0 = [scratch(f"dq0_{i}", (3, D0, H0, P)) for i in range(2)]
        dk0 = [scratch(f"dk0_{i}", (3, D0, KV0, P)) for i in range(2)]
        dk1 = [scratch(f"dk1_{i}", (3, D1, H1, P)) for i in range(2)]
        dq1 = scratch("dq1", (3, D1, H1, P))
        dkb = scratch("dkb", (NB, P))

        names = """set_io set_mask set_km set_w set_kbd set_dve set_absT set_pool sp_go mk_in mk_ok km_in
                   x_in xT_in cT_in xb_ok
                   qk_ps v_ps k1_ps qk_ev k1_ev v_ev sp0_hi sp0_r sp0_mid sp0_lo sp1_hi sp1_r sp1_mid sp1_lo
                   dq0_w dk0_w dk1_w k1_m
                   neg0T neg1T m0_split m1_split m0_in m1_in
                   ot0_ok ot1_ok ott0_ps ott1_ps rd0_ok rd1_ok at0_ok at1_ok
                   at0T_ps at1T_ps at0T_ok at1T_ok o0_ps o1_ps
                   h0_ok st0_ok mv0_ok ve0_ok rs0_ok xg_ok x1_ok x1b_ok st1_ok mv1_ok ve1_ok rs1_ok xn_ok
                   h1_ok hb_ok st2_ok mv2_ok ve2_ok rs2_ok yn_ok
                   xnT_ps xnT_ok yT_ps yT_ok q1_ps q1_ev q1_hi q1_r q1_mid q1_lo dq1_w
                   h_ps hT_ok y_ps out_ok st_even st_odd""".split()
        S = {n: sem("s_" + n) for n in names}
        q0_in, k0_in, k1_in, q1_in = (sem("s_" + n) for n in ("q0_in", "k0_in", "k1_in", "q1_in"))
        a_ps = [sem(f"s_a_ps{k}") for k in range(NT)]
        a_max = [sem(f"s_a_max{k}") for k in range(NT)]
        b_ps = [sem(f"s_b_ps{k}") for k in range(NT)]
        b_exp = [sem(f"s_b_exp{k}") for k in range(NT)]
        pv_ok = [sem(f"s_pv{k}") for k in range(NT)]

        class Has:
            def __init__(self, s):
                self.pre = 0 <= s + 1 < NB
                self.l0 = 0 <= s < NB
                self.q1 = 0 <= s - 1 < NB
                self.b1 = 0 <= s - 2 < NB
                self.mlp = 0 <= s - 3 < NB

        def steps(eng, step):
            for s in range(-1, 3):
                step(s, (s - 1) // 2, s % 2, Has(s))
            with eng.Fori(1, (NB - 2) // 2) as i:
                step(2 * i + 1, i, 1, Has(3))
                step(2 * i + 2, i, 0, Has(3))
            for s in range(NB - 1, NB + 3):
                step(s, (s - 1) // 2, s % 2, Has(s))

        def vslice(name):
            a, b = VEC[name]
            return vec[:, a:b]

        def stack(eng, done, src, dst, d, query):
            for part, reps, row in ((0, 3, 0), (1, 2, 3), (2, 1, 5)):
                if query:
                    eng.dma_start(dst[row * d:(row + reps) * d].rearrange("p h t -> p (h t)"),
                                  src[0:reps].rearrange("j d h t -> (j d) (h t)")).then_inc(done, 16)
                else:
                    one = src[part:part + 1].rearrange("j d h t -> j d (h t)")
                    eng.dma_start(dst[row * d:(row + reps) * d].rearrange("p h t -> p (h t)"),
                                  one.broadcast_to([reps, d, one.shape[2]])).then_inc(done, 16)

        def of(dram, b):
            return dram[b] if isinstance(b, int) else dram[bass.ds(b, 1)].squeeze(0)

        block = ctx.enter_context(nc.Block())

        @block.sync
        def _(sp):
            sp.sem_inc(S["st_even"], 16)
            sp.sem_inc(S["st_odd"], 16)
            for dst, src in ((xTs[:, 0], xT[0]), (w_qk[:], wqk), (col[:], cols), (cTs[:, 0], cT[0]), (w_v0[:], wv),
                             (vec[:], vecs.partition_broadcast(P)), (ident[:], eye), (xs[:, 0], x[0])):
                sp.dma_start(dst, src).then_inc(S["set_io"], 16)
            sp.dma_start(kmr[:], kmask).then_inc(S["set_km"], 16)
            sp.dma_start(maskq[:], mask.rearrange("b q k -> q b k")).then_inc(S["set_mask"], 16)
            sp.dma_start(mcur[:, 0], mask[0]).then_inc(S["mk_in"], 16)
            sp.dma_start(kmu[:, 0], kmask[0].partition_broadcast(P)).then_inc(S["km_in"], 16)
            for dst, src in ((w_k1, wk1), (w_v1, wv1), (w_o, wo), (w_q1, wq1), (w_cp, wcp), (w_fc, wfc), (w_pj, wpj)):
                sp.dma_start(dst[:], src).then_inc(S["set_w"], 16)
            sp.wait_ge(S["set_pool"], 5)
            sp.dma_start(dkb, kbias[:]).then_inc(S["set_kbd"], 16)
            sp.wait_ge(S["set_kbd"], 16)

            def step(s, stored, slot, has):
                other = 1 - slot
                if has.l0 and has.pre:
                    if not (isinstance(s, int) and s == 0):
                        sp.wait_ge(S["xb_ok"], s)
                        sp.sem_inc(S["sp_go"], 1)
                        sp.wait_ge(S["v_ps"], s + 1)
                        sp.wait_ge(S["k1_ps"], s)
                        sp.wait_ge(S["mk_ok"], s)
                        sp.wait_ge(S["k1_ev"], s)
                        sp.sem_inc(S["sp_go"], 1)
                    sp.dma_start(xTs[:, other], of(xT, s + 1)).then_inc(S["xT_in"], 16)
                    sp.dma_start(cTs[:, other], of(cT, s + 1)).then_inc(S["cT_in"], 16)
                    sp.dma_start(xs[:, other], of(x, s + 1)).then_inc(S["x_in"], 16)
                    sp.dma_start(mcur[:, other], of(mask, s + 1)).then_inc(S["mk_in"], 16)
                    sp.dma_start(kmu[:, other], of(kmask, s + 1).partition_broadcast(P)).then_inc(S["km_in"], 16)
                if has.q1:
                    sp.wait_ge(S["dk1_w"], 16 * s)
                    stack(sp, k1_in, dk1[other], KS1[other], D1, False)
                    sp.wait_ge(S["set_kbd"], 16)
                    sp.dma_start(KS1[other][R1:M1R], of(dkb, s - 1).unsqueeze(0).unsqueeze(0).broadcast_to([1, H1, P])).then_inc(S["k1_m"], 16)
                if has.l0:
                    sp.wait_ge(S["set_kbd"], 16)
                    sp.wait_ge(S["m0_split"], 4 * (s + 1))
                    for j in range(3):
                        sp.dma_start(QS0[slot][R0 + j:R0 + j + 1], m0p[:, j]).then_inc(S["m0_in"], 16)
                if has.pre:
                    sp.wait_ge(S["sp0_lo"], s + 2)
                    sp.dma_start(dq0[other].rearrange("j (c d) h t -> (d h) (j c) t", c=C),
                                 qkp[:, 0].rearrange("p j (c t) -> p (j c) t", c=C)).then_inc(S["dq0_w"], 16)
                    sp.dma_start(dk0[other].rearrange("j d h t -> (d h) j t"), qkp[0:KV0 * D0, 1, :, 0:P]).then_inc(S["dk0_w"], 16)
                if has.q1:
                    sp.wait_ge(S["q1_lo"], s)
                    sp.dma_start(dq1.rearrange("j (c d) h t -> (d h) (j c) t", c=C),
                                 q1p[:].rearrange("p j (c t) -> p (j c) t", c=C)).then_inc(S["dq1_w"], 16)
                if has.pre:
                    sp.wait_ge(S["dq0_w"], 16 * (s + 2))
                    stack(sp, q0_in, dq0[other], QS0[other], D0, True)
                if has.q1:
                    sp.wait_ge(S["dq1_w"], 16 * s)
                    if has.b1:
                        sp.wait_ge(b_ps[NT - 1], s - 1)
                    stack(sp, q1_in, dq1, QS1, D1, True)
                if has.pre:
                    sp.wait_ge(S["dk0_w"], 16 * (s + 2))
                    stack(sp, k0_in, dk0[other], KS0[other], D0, False)
                if has.mlp:
                    sp.wait_ge(S["set_kbd"], 16)
                    sp.wait_ge(S["out_ok"], s - 2)
                    sp.dma_start(of(out, s - 3), ob[:, other]).then_inc(S["st_odd" if other else "st_even"], 16)
                if has.l0:
                    sp.wait_ge(S["sp1_lo"], s + 1)
                    sp.dma_start(dk1[slot].rearrange("j (c d) h t -> (d h) (j c) t", c=C),
                                 k1p[:].rearrange("p j (c t) -> p (j c) t", c=C)).then_inc(S["dk1_w"], 16)
                if has.q1:
                    sp.wait_ge(S["m1_split"], 4 * s)
                    for j in range(3):
                        sp.dma_start(QS1[M1R + j:M1R + j + 1], m1p[:, j]).then_inc(S["m1_in"], 16)

            steps(sp, step)
            sp.wait_ge(S["st_even"], 16 * (NB // 2 + 1))
            sp.wait_ge(S["st_odd"], 16 * (NB // 2 + 1))

        @block.tensor
        def _(pe):
            mm = nc.tensor.matmul
            pe.wait_ge(S["set_io"], 16 * 8)
            pe.wait_ge(S["set_dve"], 3)
            nc.tensor.transpose(V[0][0:1, 0:P], absm[:], ident[:]).then_inc(S["set_absT"], 1)
            pe.wait_ge(S["set_dve"], 4)
            any_mask = pe.value_load(flag[:].bitcast(I32), min_val=0, max_val=2 ** 31 - 1)

            def tile_a(s, slot, k, masked, bank_of):
                if k == T0:
                    pe.wait_ge(q1_in, 48 * s)
                    pe.wait_ge(k1_in, 48 * s)
                    pe.wait_ge(S["k1_m"], 16 * s)
                if bank_of is not None:
                    pe.wait_ge(a_max[bank_of], s + 1 if bank_of < T0 else s)
                for j in range(TH):
                    if k < T0:
                        last = mm(A[k % 2][:, j * P:(j + 1) * P], QS0[slot][0:R0, k * G0 + j], KS0[slot][0:R0, k],
                                  start=j == 0, stop=not masked, skip_group_check=True)
                    else:
                        h = (k - T0) * TH + j
                        last = mm(A[k % 2][:, j * P:(j + 1) * P], QS1[0:M1R, h], KS1[1 - slot][0:M1R, h],
                                  start=j == 0, stop=True, skip_group_check=True)
                if masked and k < T0:
                    last = mm(A[k % 2][:].rearrange("p (g k) -> p g k", g=G0), ident[:],
                              mcl[slot][:].unsqueeze(1).broadcast_to([P, G0, P]), start=False, stop=True, skip_group_check=True)
                last.then_inc(a_ps[k], 1)

            def tile_b(s, slot, k, masked, bank_of):
                if bank_of is not None:
                    pe.wait_ge(b_exp[bank_of], s + 1 if bank_of < T0 else s - 1)
                if k < T0:
                    last = mm(B[k % 2][:], KS0[slot][0:M0R, k], QS0[slot][0:M0R, k * G0:(k + 1) * G0],
                              start=True, stop=not masked, skip_group_check=True)
                    if masked:
                        for g in range(G0):
                            last = mm(B[k % 2][:, g * P:(g + 1) * P], mcl[slot][:], ident[:], start=False, stop=True,
                                      skip_group_check=True)
                else:
                    for j in range(TH):
                        h = (k - T0) * TH + j
                        last = mm(B[k % 2][:, j * P:(j + 1) * P], KS1[slot][0:M1E, h], QS1[0:M1E, h],
                                  start=j == 0, stop=True, skip_group_check=True)
                last.then_inc(b_ps[k], 1)

            def tile_pv(s, slot, k):
                pe.wait_ge(b_exp[k], s + 1 if k < T0 else s - 1)
                if k < T0:
                    q = k % TH * W
                    last = mm(V[k // TH][q:q + W, :], V0[slot][:, k], prob[k % NP][:].rearrange("p h t -> p (h t)"),
                              start=True, stop=True, skip_group_check=True)
                else:
                    for j in range(TH):
                        h = (k - T0) * TH + j
                        last = mm(V[0][j * W:(j + 1) * W, (k - T0) * P:(k - T0 + 1) * P], V1[slot][:, h], prob[k % NP][:, j],
                                  start=True, stop=True, skip_group_check=True)
                last.then_inc(pv_ok[k], 1)

            def flip(dst, src, done):
                for c in range(C):
                    last = nc.tensor.transpose(dst[:, c * P:(c + 1) * P], src[:, c * P:(c + 1) * P], ident[:])
                last.then_inc(done, 1)

            def tokens_out(dst, lhs, w, start_first=True):
                chunks = w.shape[1]
                for c in range(chunks):
                    last = mm(dst, lhs[:, c], w[:, c], start=c == 0 and start_first, stop=c == chunks - 1, skip_group_check=True)
                return last

            def dims_out(dst, w, rhs, m):
                for c in range(C):
                    last = mm(dst, w[:, c, m * P:(m + 1) * P], rhs[:, c], start=m == 0 and c == 0, stop=c == C - 1, skip_group_check=True)
                return last

            def turn(dst, src, done):
                for t in range(TH):
                    last = nc.tensor.transpose(dst[:, t * P:(t + 1) * P], src[:, t * P:(t + 1) * P], ident[:])
                last.then_inc(done, 1)

            def step(s, stored, slot, has):
                other = 1 - slot

                def mlp_up(a):
                    if has.mlp:
                        if a == 0:
                            pe.wait_ge(S["yT_ok"], s - 2)
                        for m in range(TH):
                            r = a * TH + m
                            for c in range(C):
                                last = mm(B[a][:, m * P:(m + 1) * P], w_fc[:, c, r * P:(r + 1) * P], yT[:, c],
                                          start=m == 0 and c == 0, stop=c == C - 1, skip_group_check=True)
                        last.then_inc(S["h_ps"], 1)

                def mlp_down(a):
                    if has.mlp:
                        if a == 0:
                            pe.wait_ge(S["hT_ok"], s - 2)
                            if has.l0:
                                pe.wait_ge(S["k1_ev"], s + 1)
                            else:
                                pe.wait_ge(S["h1_ok"], s - 2)
                        for m in range(a * TH, (a + 1) * TH):
                            last = mm(M[1][:, 0:D], hT[:, m], w_pj[:, m], start=m == 0, stop=m == FC - 1, skip_group_check=True)
                        if a == 1:
                            last.then_inc(S["y_ps"], 1)

                def turn0(a, n):
                    pe.wait_ge(S["ot0_ok"], 2 * n - 1 + a)
                    turn(V[a], ot0[:, a], S["ott0_ps"])

                def at0_flip():
                    pe.wait_ge(S["at0_ok"], 2 * s)
                    if has.b1:
                        pe.wait_ge(S["m1_split"], 4 * (s - 1))
                    else:
                        pe.wait_ge(S["k1_ev"], s)
                    flip(M[1], at0[:].rearrange("p h d -> p (h d)"), S["at0T_ps"])

                def out0():
                    pe.wait_ge(S["at0T_ok"], s)
                    if has.mlp:
                        pe.wait_ge(S["yT_ok"], s - 2)
                    elif has.l0:
                        pe.wait_ge(S["v_ev"], s + 1)
                    tokens_out(M[0][:, 0:D], at0T, w_o).then_inc(S["o0_ps"], 1)

                def project_qk():
                    if has.l0:
                        pe.wait_ge(S["xT_in"], 16 * (s + 1))
                        pe.wait_ge(S["cT_in"], 16 * (s + 1))
                    if isinstance(s, int) and s == 0:
                        pe.wait_ge(S["qk_ev"], s + 1)
                    for m in range(C):
                        dims_out(M[1][:, m * P:(m + 1) * P], w_qk, xTs[:, other], m)
                    for c in range(C):
                        last = mm(M[1][:, D:D + P], w_qk[:, c, D:D + P], cTs[:, other, c], start=False, stop=c == C - 1,
                                  skip_group_check=True)
                    last.then_inc(S["qk_ps"], 1)

                def xn_flip():
                    pe.wait_ge(S["xn_ok"], s)
                    if has.pre:
                        pe.wait_ge(S["qk_ev"], s + 2)
                    flip(M[1], xn[:], S["xnT_ps"])

                def project_q1():
                    pe.wait_ge(S["xnT_ok"], s)
                    pe.wait_ge(S["h0_ok"], s)
                    for m in range(C):
                        last = dims_out(M[0][:, m * P:(m + 1) * P], w_q1, xnT, m)
                    last.then_inc(S["q1_ps"], 1)

                def negated(src, dst, last_max, n, done):
                    pe.wait_ge(last_max, n)
                    nc.tensor.transpose(dst[:, 0:P], src[:], ident[:]).then_inc(done, 1)

                def first_half(masked):
                    a = lambda k: tile_a(s, slot, k, masked, k - 2 if k >= 2 else None) if has.l0 else None
                    b = lambda k: tile_b(s, slot, k, False, k - 2 if k >= T0 + 2 else None) if has.b1 else None
                    pv = lambda k: tile_pv(s, slot, k) if has.b1 else None
                    if has.l0:
                        pe.wait_ge(q0_in, 48 * (s + 1))
                        pe.wait_ge(k0_in, 48 * (s + 1))
                        pe.wait_ge(S["mk_ok"], s + 1)
                    a(0)
                    if has.q1:
                        turn0(1, s)
                    a(1)
                    mlp_up(0)
                    if has.q1:
                        at0_flip()
                    a(2)
                    mlp_up(1)
                    if has.q1:
                        out0()
                    a(3)
                    if has.pre:
                        project_qk()
                    a(4)
                    if has.b1:
                        pe.wait_ge(S["m1_in"], 48 * (s - 1))
                        if has.mlp:
                            pe.wait_ge(S["hT_ok"], s - 2)
                    b(T0)
                    b(T0 + 1)
                    a(5)
                    pv(T0)
                    b(T0 + 2)
                    a(6)
                    pv(T0 + 1)
                    b(T0 + 3)
                    if has.q1:
                        xn_flip()
                    a(7)
                    if has.q1:
                        project_q1()
                    pv(T0 + 2)
                    if has.l0:
                        negated(negm0, V[1], a_max[T0 - 1], s + 1, S["neg0T"])
                    pv(T0 + 3)

                if has.l0:
                    with pe.If(any_mask > 0):
                        first_half(True)
                    with pe.Else():
                        first_half(False)
                    pe.nop()
                else:
                    first_half(False)

                if has.l0:
                    if isinstance(s, int) and s == 0:
                        pe.wait_ge(S["set_w"], 16 * 7)
                        pe.wait_ge(S["qk_ev"], s + 2)
                    else:
                        pe.wait_ge(S["xnT_ok"], s)
                    for m in range(C):
                        last = dims_out(M[1][:, m * P:(m + 1) * P], w_k1, cTs[:, slot], m)
                    last.then_inc(S["k1_ps"], 1)
                    if isinstance(s, int) and s == 0:
                        pe.wait_ge(S["v_ev"], s + 1)
                    else:
                        pe.wait_ge(S["q1_ev"], s)
                if has.pre:
                    last = tokens_out(M[0][:, 0:KV0 * D0], cTs[:, other], w_v0)
                if has.l0:
                    last = tokens_out(M[0][:, P:P + D], cTs[:, slot], w_v1, not has.pre)
                if has.l0 or has.pre:
                    last.then_inc(S["v_ps"], 1)
                mlp_down(0)
                if has.b1:
                    pe.wait_ge(S["ot1_ok"], s - 1)
                    turn(V[0], ot1[:], S["ott1_ps"])
                mlp_down(1)
                if has.b1:
                    pe.wait_ge(S["at1_ok"], s - 1)
                    if has.l0:
                        pe.wait_ge(S["v_ev"], s + 2)
                    elif has.q1:
                        pe.wait_ge(S["q1_ev"], s)
                    else:
                        pe.wait_ge(S["yT_ok"], s - 2)
                    flip(M[0], at1[:].rearrange("p h d -> p (h d)"), S["at1T_ps"])

                def second_half(masked):
                    a = lambda k: tile_a(s, slot, k, False, k - 2 if k >= T0 + 2 else None) if has.q1 else None
                    b = lambda k: tile_b(s, slot, k, masked, k - 2 if k >= 2 else None) if has.l0 else None
                    pv = lambda k: tile_pv(s, slot, k) if has.l0 else None
                    if has.l0:
                        pe.wait_ge(S["m0_in"], 48 * (s + 1))
                    b(0)
                    b(1)
                    pv(0)
                    b(2)
                    if has.b1:
                        pe.wait_ge(S["at1T_ok"], s - 1)
                        if has.mlp:
                            pe.wait_ge(S["out_ok"], s - 2)
                        elif has.l0:
                            pe.wait_ge(S["k1_ev"], s + 1)
                        tokens_out(M[1][:, 0:D], at1T, w_cp).then_inc(S["o1_ps"], 1)
                    pv(1)
                    b(3)
                    pv(2)
                    b(4)
                    a(T0)
                    pv(3)
                    b(5)
                    a(T0 + 1)
                    pv(4)
                    b(6)
                    a(T0 + 2)
                    pv(5)
                    b(7)
                    if has.l0:
                        turn0(0, s + 1)
                    pv(6)
                    if has.b1:
                        pe.wait_ge(S["yn_ok"], s - 1)
                        flip(M[0], yn[:], S["yT_ps"])
                    a(T0 + 3)
                    pv(7)
                    if has.q1:
                        if has.b1:
                            pe.wait_ge(S["h1_ok"], s - 1)
                        negated(negm1, M[1], a_max[NT - 1], s, S["neg1T"])

                if has.l0:
                    with pe.If(any_mask > 0):
                        second_half(True)
                    with pe.Else():
                        second_half(False)
                    pe.nop()
                else:
                    second_half(False)

            steps(pe, step)

        @block.vector
        def _(dve):
            v = nc.vector
            v.memset(qk32[:], 0.0)
            v.memset(negm0[:], 0.0)
            v.memset(negm1[:], 0.0)
            for i in range(2):
                v.memset(KS0[i][32:2 * 32], 1.0)
                v.memset(KS1[i][R1:P], 1.0)
            v.memset(QS1[R1:P], 1.0)
            for i in range(2):
                v.memset(V0[i][:], 0.0)
                v.memset(V1[i][:], 0.0).then_inc(S["set_dve"], 1)
            dve.wait_ge(S["set_dve"], 2)
            for i in range(2):
                v.memset(V0[i][:, :, D0:D0 + 1], 1.0)
                v.memset(V1[i][:, :, D1:D1 + 1], 1.0)
            dve.wait_ge(S["set_mask"], 16)
            v.tensor_reduce(absm[:], maskq[:].rearrange("p b k -> p (b k)"), AX.X, ALU.max, apply_absolute_value=True)\
                .then_inc(S["set_dve"], 1)
            dve.wait_ge(S["set_absT"], 1)
            v.tensor_reduce(flag[:], V[0][0:1, 0:P], AX.X, ALU.max).then_inc(S["set_dve"], 1)

            def stats(x_, ready, n, st, done):
                dve.wait_ge(ready, n)
                v.bn_stats(st[:], x_).then_inc(done, 1)

            def mean_var(n, st, mv, ve, eps, st_ok, mv_ok, ve_ok):
                dve.wait_ge(S["set_dve"], 2)
                dve.wait_ge(st_ok, n)
                v.bn_aggr(mv[:], st[:]).then_inc(mv_ok, 1)
                dve.wait_ge(mv_ok, n)
                v.tensor_scalar(ve[:], mv[:, 1:2], eps, None, ALU.add).then_inc(ve_ok, 1)

            def split_max(src, ready, n, mp, mr, done):
                dve.wait_ge(ready, n)
                v.tensor_copy(mp[:, 0], src).then_inc(done, 1)
                dve.wait_ge(done, 4 * n - 3)
                v.tensor_tensor(mr[:], src, mp[:, 0], ALU.subtract).then_inc(done, 1)
                dve.wait_ge(done, 4 * n - 2)
                v.tensor_copy(mp[:, 1], mr[:]).then_inc(done, 1)
                dve.wait_ge(done, 4 * n - 1)
                v.tensor_tensor(mp[:, 2], mr[:], mp[:, 1], ALU.subtract).then_inc(done, 1)

            def step(s, stored, slot, has):
                other = 1 - slot

                def top(k):
                    if has.l0 if k < T0 else has.q1:
                        dve.wait_ge(a_ps[k], s + 1 if k < T0 else s)
                        dst = negm0[:, k * TH:(k + 1) * TH] if k < T0 else negm1[:, (k - T0) * TH:(k - T0 + 1) * TH]
                        v.tensor_reduce(dst, A[k % 2][:].rearrange("p (g k) -> p g k", g=TH), AX.X, ALU.max, negate=True)\
                            .then_inc(a_max[k], 1)

                def divide0(a, n):
                    pv = V[a][:].rearrange("p (g j w) -> p j g w", j=TH, w=W)
                    r = rd0[:, a].rearrange("p (j g) o -> p j g o", g=G0)
                    dve.wait_ge(S["ott0_ps"], 2 * n - 1 + a)
                    v.reciprocal(r, pv[:, :, :, D0:D0 + 1]).then_inc(S["rd0_ok"], 1)
                    dve.wait_ge(S["rd0_ok"], 2 * n - 1 + a)
                    v.tensor_tensor(at0[:, a * H0 // 2:(a + 1) * H0 // 2].rearrange("p (j g) d -> p j g d", g=G0),
                                    pv[:, :, :, 0:D0], r.broadcast_to([P, TH, G0, D0]), ALU.mult).then_inc(S["at0_ok"], 1)

                if has.q1:
                    divide0(1, s)
                top(0)
                top(1)
                top(2)
                if has.q1:
                    dve.wait_ge(S["o0_ps"], s)
                    dve.wait_ge(S["xb_ok"], s)
                    v.tensor_tensor(h0[:], M[0][:, 0:D], xb[:, other], ALU.add).then_inc(S["h0_ok"], 1)
                    stats(h0[:], S["h0_ok"], s, st0, S["st0_ok"])
                top(3)
                if has.q1:
                    mean_var(s, st0, mv0, ve0, EPS0, S["st0_ok"], S["mv0_ok"], S["ve0_ok"])
                    v.scalar_tensor_tensor(xg[:], h0[:], mv0[:, 0:1], vslice("gamma"), ALU.subtract, ALU.mult).then_inc(S["xg_ok"], 1)
                top(4)
                if has.q1:
                    dve.wait_ge(S["rs0_ok"], s)
                    dve.wait_ge(S["xg_ok"], s)
                    v.scalar_tensor_tensor(x1[:], xg[:], rs0[:], vslice("beta"), ALU.mult, ALU.add).then_inc(S["x1_ok"], 1)
                    stats(x1[:], S["x1_ok"], s, st1, S["st1_ok"])
                top(5)
                if has.q1:
                    mean_var(s, st1, mv1, ve1, EPS1, S["st1_ok"], S["mv1_ok"], S["ve1_ok"])
                top(6)
                if has.q1:
                    dve.wait_ge(S["rs1_ok"], s)
                    v.tensor_scalar(xn[:], x1[:], mv1[:, 0:1], rs1[:], ALU.subtract, ALU.mult).then_inc(S["xn_ok"], 1)
                top(7)
                if has.l0:
                    split_max(V[1][0:H0, 0:P], S["neg0T"], s + 1, m0p, m0r, S["m0_split"])
                    dve.wait_ge(S["k1_ps"], s + 1)
                    dve.wait_ge(S["km_in"], 16 * (s + 1))
                    if not (isinstance(s, int) and s == 0):
                        dve.wait_ge(S["sp1_lo"], s)
                    for c in range(C):
                        last = v.scalar_tensor_tensor(k32[:, c * P:(c + 1) * P], M[1][:, c * P:(c + 1) * P],
                                                      col[:, COL["k1"] + c:COL["k1"] + c + 1], kmu[:, slot], ALU.add, ALU.mult)
                    last.then_inc(S["k1_ev"], 1)
                if has.q1:
                    dve.wait_ge(S["q1_hi"], s)
                    v.tensor_tensor(q1r[:], q32[:], q1p[:, 0], ALU.subtract).then_inc(S["q1_r"], 1)
                if has.l0 or has.pre:
                    dve.wait_ge(S["v_ps"], s + 2)
                    if not has.l0:
                        dve.wait_ge(S["set_io"], 16 * 8)
                if has.pre:
                    last = v.tensor_tensor(V0[other][:, :, 0:D0], M[0][:, 0:KV0 * D0].rearrange("p (h d) -> p h d", d=D0),
                                           vslice("v0").rearrange("p (h d) -> p h d", d=D0), ALU.add)
                if has.l0:
                    last = v.tensor_tensor(V1[slot][:, :, 0:D1], M[0][:, P:P + D].rearrange("p (h d) -> p h d", d=D1),
                                           vslice("v1").rearrange("p (h d) -> p h d", d=D1), ALU.add)
                if has.l0 or has.pre:
                    last.then_inc(S["v_ev"], 1)
                if has.q1:
                    dve.wait_ge(S["q1_mid"], s)
                    v.tensor_tensor(q1p[:, 2], q1r[:], q1p[:, 1], ALU.subtract).then_inc(S["q1_lo"], 1)
                if has.pre:
                    dve.wait_ge(S["mk_in"], 16 * (s + 2))
                    v.tensor_scalar(mcl[other][:], mcur[:, other], LOWEST, None, ALU.max).then_inc(S["mk_ok"], 1)
                if has.b1:
                    pv1 = V[0][:].rearrange("p (h w) -> p h w", w=W)
                    dve.wait_ge(S["ott1_ps"], s - 1)
                    v.reciprocal(rd1[:], pv1[:, :, D1:D1 + 1]).then_inc(S["rd1_ok"], 1)
                    dve.wait_ge(S["rd1_ok"], s - 1)
                    v.tensor_tensor(at1[:], pv1[:, :, 0:D1], rd1[:].broadcast_to([P, H1, D1]), ALU.mult).then_inc(S["at1_ok"], 1)
                if has.mlp:
                    dve.wait_ge(S["y_ps"], s - 2)
                    dve.wait_ge(S["hb_ok"], s - 2)
                    dve.wait_ge(S["st_odd" if other else "st_even"], 16 * stored)
                    v.tensor_tensor(ob[:, other], M[1][:, 0:D], hb[:], ALU.add).then_inc(S["out_ok"], 1)
                if has.b1:
                    dve.wait_ge(S["o1_ps"], s - 1)
                    dve.wait_ge(S["x1b_ok"], s - 1)
                    v.tensor_tensor(h1[:], M[1][:, 0:D], x1b[:, slot], ALU.add).then_inc(S["h1_ok"], 1)
                    stats(h1[:], S["h1_ok"], s - 1, st2, S["st2_ok"])
                top(T0)
                if has.b1:
                    mean_var(s - 1, st2, mv2, ve2, EPS1, S["st2_ok"], S["mv2_ok"], S["ve2_ok"])
                top(T0 + 1)
                top(T0 + 2)
                if has.l0:
                    divide0(0, s + 1)
                if has.b1:
                    dve.wait_ge(S["rs2_ok"], s - 1)
                    v.tensor_scalar(yn[:], h1[:], mv2[:, 0:1], rs2[:], ALU.subtract, ALU.mult).then_inc(S["yn_ok"], 1)
                top(T0 + 3)
                if has.q1:
                    split_max(M[1][0:H1, 0:P], S["neg1T"], s, m1p, m1r, S["m1_split"])

            steps(dve, step)

        @block.scalar
        def _(act):
            a = nc.scalar.activation
            act.wait_ge(S["set_io"], 16 * 8)
            act.wait_ge(S["set_pool"], 3)

            def step(s, stored, slot, has):
                def exp(k):
                    if has.l0 if k < T0 else has.b1:
                        act.wait_ge(b_ps[k], s + 1 if k < T0 else s - 1)
                        if k >= T0:
                            if has.q1:
                                act.wait_ge(pv_ok[k - NP], s)
                        elif k >= NP:
                            act.wait_ge(pv_ok[k - NP], s + 1)
                        elif has.b1:
                            act.wait_ge(pv_ok[k + T0], s - 1)
                        a(prob[k % NP][:].rearrange("p h t -> p (h t)"), B[k % 2][:], ACT.Exp).then_inc(b_exp[k], 1)

                def sums0(half_):
                    act.wait_ge(pv_ok[(half_ + 1) * TH - 1], s + 1)
                    a(ot0[:, half_], V[half_][:], ACT.Copy).then_inc(S["ot0_ok"], 1)

                if has.q1:
                    act.wait_ge(S["at0T_ps"], s)
                    a(at0T[:].rearrange("p c t -> p (c t)"), M[1][:, 0:D], ACT.Copy).then_inc(S["at0T_ok"], 1)
                if has.mlp:
                    for m in range(FC):
                        if m % TH == 0:
                            act.wait_ge(S["h_ps"], 2 * s - 5 + m // TH)
                        last = a(hT[:, m], B[m // TH][:, (m % TH) * P:(m % TH + 1) * P], ACT.Gelu_apprx_tanh,
                                 bias=col[:, COL["fc"] + m:COL["fc"] + m + 1])
                    last.then_inc(S["hT_ok"], 1)
                if has.pre:
                    act.wait_ge(S["qk_ps"], s + 2)
                    if has.l0:
                        act.wait_ge(S["sp0_lo"], s + 1)
                    else:
                        act.wait_ge(S["set_dve"], 2)
                    for c in range(C):
                        a(qk32[:, 0, c * P:(c + 1) * P], M[1][:, c * P:(c + 1) * P], ACT.Identity, bias=sbias[:, c:c + 1], scale=S0)
                    a(qk32[:, 1, 0:P], M[1][:, D:D + P], ACT.Identity, bias=col[:, COL["k0"]:COL["k0"] + 1]).then_inc(S["qk_ev"], 1)
                    act.wait_ge(S["qk_ev"], s + 2)
                    if has.l0:
                        act.wait_ge(S["dq0_w"], 16 * (s + 1))
                        act.wait_ge(S["dk0_w"], 16 * (s + 1))
                    a(qkp[:, :, 0], qk32[:], ACT.Copy).then_inc(S["sp0_hi"], 1)
                exp(T0)
                exp(T0 + 1)
                if has.pre:
                    act.wait_ge(S["sp0_r"], s + 2)
                    a(qkp[:, :, 1], qkr[:], ACT.Copy).then_inc(S["sp0_mid"], 1)
                exp(T0 + 2)
                if has.q1:
                    act.wait_ge(S["xnT_ps"], s)
                    for c in range(C):
                        last = a(xnT[:, c], M[1][:, c * P:(c + 1) * P], ACT.Identity, bias=col[:, COL["b1"] + c:COL["b1"] + c + 1],
                                 scale=col[:, COL["w1"] + c:COL["w1"] + c + 1])
                    last.then_inc(S["xnT_ok"], 1)
                exp(T0 + 3)
                if has.q1:
                    act.wait_ge(S["q1_ps"], s)
                    for c in range(C):
                        last = a(q32[:, c * P:(c + 1) * P], M[0][:, c * P:(c + 1) * P], ACT.Identity, bias=sbias[:, 2 + c:3 + c], scale=S1)
                    last.then_inc(S["q1_ev"], 1)
                    act.wait_ge(S["q1_ev"], s)
                    if has.b1:
                        act.wait_ge(S["dq1_w"], 16 * (s - 1))
                    a(q1p[:, 0], q32[:], ACT.Copy).then_inc(S["q1_hi"], 1)
                if has.b1:
                    act.wait_ge(pv_ok[NT - 1], s - 1)
                    a(ot1[:], V[0][:], ACT.Copy).then_inc(S["ot1_ok"], 1)
                if has.q1:
                    act.wait_ge(S["q1_r"], s)
                    a(q1p[:, 1], q1r[:], ACT.Copy).then_inc(S["q1_mid"], 1)
                if has.l0:
                    act.wait_ge(S["k1_ev"], s + 1)
                    if not (isinstance(s, int) and s == 0):
                        act.wait_ge(S["dk1_w"], 16 * s)
                    a(k1p[:, 0], k32[:], ACT.Copy).then_inc(S["sp1_hi"], 1)
                if has.b1:
                    act.wait_ge(S["at1T_ps"], s - 1)
                    a(at1T[:].rearrange("p c t -> p (c t)"), M[0][:, 0:D], ACT.Copy).then_inc(S["at1T_ok"], 1)
                exp(0)
                exp(1)
                if has.l0:
                    act.wait_ge(S["sp1_r"], s + 1)
                    a(k1p[:, 1], k1r[:], ACT.Copy).then_inc(S["sp1_mid"], 1)
                for k in range(2, 6):
                    exp(k)
                if has.l0:
                    sums0(0)
                exp(6)
                exp(7)
                if has.b1:
                    act.wait_ge(S["yT_ps"], s - 1)
                    for c in range(C):
                        last = a(yT[:, c], M[0][:, c * P:(c + 1) * P], ACT.Identity, bias=col[:, COL["b2"] + c:COL["b2"] + c + 1],
                                 scale=col[:, COL["w2"] + c:COL["w2"] + c + 1])
                    last.then_inc(S["yT_ok"], 1)
                if has.l0:
                    sums0(1)

            steps(act, step)

        @block.gpsimd
        def _(pool):
            g = nc.gpsimd
            g.memset(half[:], -0.5).then_inc(S["set_pool"], 1)
            pool.wait_ge(S["set_pool"], 1)
            pool.wait_ge(S["set_io"], 16 * 8)
            g.tensor_scalar(sbias[:, 0:2], col[:, COL["q0"]:COL["q0"] + 2], S0, None, ALU.mult).then_inc(S["set_pool"], 1)
            pool.wait_ge(S["set_pool"], 2)
            g.tensor_scalar(sbias[:, 2:4], col[:, COL["q1"]:COL["q1"] + 2], S1, None, ALU.mult).then_inc(S["set_pool"], 1)
            pool.wait_ge(S["set_km"], 16)
            g.tensor_copy(kmf[:], kmr[:]).then_inc(S["set_pool"], 1)
            pool.wait_ge(S["set_pool"], 4)
            g.tensor_scalar(kbias[:], kmf[:], 1.0, MASKED, ALU.subtract, ALU.mult).then_inc(S["set_pool"], 1)

            def inverse_root(ve, rs, n, stats_done, t_out):
                pool.wait_ge(stats_done, n)
                g.tensor_tensor(rs[:], ve[:], half[:], ALU.pow).then_inc(S[t_out], 1)

            def step(s, stored, slot, has):
                other = 1 - slot
                if has.q1:
                    inverse_root(ve0, rs0, s, S["ve0_ok"], "rs0_ok")
                if has.pre:
                    pool.wait_ge(S["sp0_hi"], s + 2)
                    g.tensor_tensor(qkr[:], qk32[:], qkp[:, :, 0], ALU.subtract).then_inc(S["sp0_r"], 1)
                if has.q1:
                    inverse_root(ve1, rs1, s, S["ve1_ok"], "rs1_ok")
                if has.pre:
                    pool.wait_ge(S["sp0_mid"], s + 2)
                    g.tensor_tensor(qkp[:, :, 2], qkr[:], qkp[:, :, 1], ALU.subtract).then_inc(S["sp0_lo"], 1)
                if has.q1:
                    g.tensor_tensor(x1b[:, other], x1[:], vslice("cp"), ALU.add).then_inc(S["x1b_ok"], 1)
                if has.l0:
                    if not (isinstance(s, int) and s == 0):
                        pool.wait_ge(S["x_in"], 16 * s)
                    g.tensor_tensor(xb[:, slot], xs[:, slot], vslice("bo"), ALU.add).then_inc(S["xb_ok"], 1)
                    pool.wait_ge(S["sp1_hi"], s + 1)
                    g.tensor_tensor(k1r[:], k32[:], k1p[:, 0], ALU.subtract).then_inc(S["sp1_r"], 1)
                    pool.wait_ge(S["sp1_mid"], s + 1)
                    g.tensor_tensor(k1p[:, 2], k1r[:], k1p[:, 1], ALU.subtract).then_inc(S["sp1_lo"], 1)
                if has.b1:
                    inverse_root(ve2, rs2, s - 1, S["ve2_ok"], "rs2_ok")
                    g.tensor_tensor(hb[:], h1[:], vslice("pb"), ALU.add).then_inc(S["hb_ok"], 1)

            steps(pool, step)


_OUT = (NB, P, D)


def kernel(**inputs):
    import numpy as np
    import concourse.bacc as bacc
    from concourse import mybir as mb
    from concourse.bass_utils import run_bass_kernel_spmd as run

    g = {k: np.asarray(v) for k, v in inputs.items()}

    def rows(w):
        return w.reshape(-1, P, w.shape[1]).transpose(1, 0, 2)

    def heads_inner(w, h, d):
        return w.reshape(w.shape[:-1] + (h, d)).swapaxes(-1, -2).reshape(w.shape)

    def column(b):
        return b.reshape(-1, P).T

    L0, L1 = "L0_xattn_", "L1_xattn_"
    wk0 = heads_inner(g[L0 + "Wk"], KV0, D0)
    bk0 = heads_inner(g[L0 + "bk"], KV0, D0)
    turned = lambda t: t.transpose(0, 2, 1).reshape(NB, C, P, P).transpose(0, 2, 1, 3)
    data = dict(
        x=g["x"], xT=turned(g["x"]), cT=turned(g["ctx_2048"]),
        mask=g["mask_Bx1xSxS2_ff0"].reshape(NB, P, P), kmask=g["mask_BxS2_bf1"],
        eye=np.eye(P, dtype=np.float32),
        cols=np.concatenate([
            column(heads_inner(g[L0 + "bq"], H0, D0)), column(np.concatenate([bk0, bk0])),
            column(heads_inner(g[L1 + "k_b"], H1, D1)), column(heads_inner(g[L1 + "q_b"], H1, D1)),
            column(g[L1 + "ln1_w"]), column(g[L1 + "ln1_b"]), column(g[L1 + "ln2_w"]), column(g[L1 + "ln2_b"]),
            column(g[L1 + "fc_b"])], axis=1),
        vecs=np.concatenate([g[L0 + "bv"], g[L1 + "v_b"], g[L0 + "bo"], g[L0 + "gamma"], g[L0 + "beta"],
                             g[L1 + "cproj_b"], g[L1 + "proj_b"]]),
        wqk=rows(np.concatenate([heads_inner(g[L0 + "Wq"], H0, D0), wk0, wk0], axis=1)),
        wv=rows(g[L0 + "Wv"]), wo=rows(g[L0 + "Wo"]),
        wk1=rows(heads_inner(g[L1 + "k_w"], H1, D1)), wq1=rows(heads_inner(g[L1 + "q_w"], H1, D1)),
        wv1=rows(g[L1 + "v_w"]), wcp=rows(g[L1 + "cproj_w"]), wfc=rows(g[L1 + "fc_w"]), wpj=rows(g[L1 + "proj_w"]),
    )
    nc = bacc.Bacc("TRN2", target_bir_lowering=False, num_devices=1)
    arrays, args = {}, {}
    for name, a in data.items():
        a = np.ascontiguousarray(a)
        arrays["in_" + name] = a
        args[name] = nc.dram_tensor("in_" + name, a.shape, mb.dt.from_np(a.dtype), kind="ExternalInput").ap()
    args["out"] = nc.dram_tensor("out_0", _OUT, F32, kind="ExternalOutput").ap()
    build(nc, **args)
    r = run(nc, [arrays], core_ids=[0])
    return r.results[0]["out_0"]
```

```python
import concourse.bass as bass
from concourse import mybir
from contextlib import ExitStack

F32 = mybir.dt.float32
BF16 = mybir.dt.bfloat16
I32 = mybir.dt.int32
ALU = mybir.AluOpType
ACT = mybir.ActivationFunctionType
AX = mybir.AxisListType

NB = 8
P = 128
D = 256
C = D // P
H0, KV0, D0 = 32, 8, 8
H1, D1 = 16, 16
G0 = H0 // KV0
FF = 4 * D
FC = FF // P
R0 = 6 * D0
R1 = 6 * D1
M0R = R0 + 3
M1R = R1 + 1
M1E = M1R + 3
S0 = float(D0) ** -0.5
S1 = float(D1) ** -0.5
EPS0, EPS1 = 1e-6, 1e-5
MASKED = 2.0 ** 100
LOWEST = -3.0e38
TH = 4
T0 = H0 // TH
T1 = H1 // TH
NT = T0 + T1
W = 32
NP = 4

COL = dict(q0=0, k0=2, k1=3, q1=5, w1=7, b1=9, w2=11, b2=13, fc=15)
NCOL = 15 + FC
VEC, _at = {}, 0
for _name, _n in (("v0", KV0 * D0), ("v1", D), ("bo", D), ("gamma", D), ("beta", D), ("cp", D), ("pb", D)):
    VEC[_name] = (_at, _at + _n)
    _at += _n
NVEC = _at


def build(nc, x, xT, cT, mask, kmask, eye, cols, vecs, wqk, wv, wo, wk1, wq1, wcp, wfc, wpj, out):
    with ExitStack() as ctx:
        def sb(name, shape, dt=F32):
            return ctx.enter_context(nc.sbuf_tensor(name, shape, dt))

        def ps(name, shape):
            return ctx.enter_context(nc.psum_tensor(name, shape, F32))

        def sem(name):
            return ctx.enter_context(nc.semaphore(name))

        ident = sb("ident", [P, P])
        col = sb("col", [P, NCOL])
        vec = sb("vec", [P, NVEC])
        w_qk = sb("w_qk", [P, C, D + P])
        w_v = sb("w_v", [P, C, KV0 * D0 + D])
        w_o = sb("w_o", [P, C, D])
        w_k1 = sb("w_k1", [P, C, D])
        w_q1 = sb("w_q1", [P, C, D])
        w_cp = sb("w_cp", [P, C, D])
        w_fc = sb("w_fc", [P, C, FF])
        w_pj = sb("w_pj", [P, FC, D])
        maskq = sb("maskq", [P, NB, P])
        mcur = sb("mcur", [P, 2, P])
        mcl = [sb(f"mcl{i}", [P, P]) for i in range(2)]
        kmu = sb("kmu", [P, 2, P], mybir.dt.uint8)
        kmr = sb("kmr", [NB, P], mybir.dt.uint8)
        kbias = sb("kbias", [NB, P], BF16)
        absm = sb("absm", [P, 1])
        flag = sb("flag", [1, 1])
        warm = sb("warm", [P, 1])
        half = sb("half", [P, 1])
        xs = sb("xs", [P, 2, D])
        xTs = sb("xTs", [P, 2, C, P])
        cTs = sb("cTs", [P, 2, C, P])
        xb = sb("xb", [P, 2, D])
        qk32 = sb("qk32", [P, 2, 2 * P])
        qkr = sb("qkr", [P, 2, 2 * P])
        qkp = sb("qkp", [P, 2, 3, 2 * P], BF16)
        k32 = sb("k32", [P, 2 * P])
        k1r = sb("k1r", [P, 2 * P])
        k1p = sb("k1p", [P, 3, 2 * P], BF16)
        q32 = sb("q32", [P, 2 * P])
        q1r = sb("q1r", [P, 2 * P])
        q1p = sb("q1p", [P, 3, 2 * P], BF16)
        QS0 = [sb(f"QS0_{i}", [P, H0, P], BF16) for i in range(2)]
        KS0 = [sb(f"KS0_{i}", [P, KV0, P], BF16) for i in range(2)]
        KS1 = [sb(f"KS1_{i}", [P, H1, P], BF16) for i in range(2)]
        QS1 = sb("QS1", [P, H1, P], BF16)
        V0 = sb("V0_", [P, KV0, W])
        V1 = [sb(f"V1_{i}", [P, H1, W]) for i in range(2)]
        ot0 = sb("ot0", [P, 2, TH * P])
        ot1 = sb("ot1", [P, TH * P])
        negm0 = sb("negm0", [P, P])
        negm1 = sb("negm1", [P, P])
        sbias = sb("sbias", [P, 4])
        kmf = sb("kmf", [NB, P])
        m0r = sb("m0r", [H0, P])
        m0p = sb("m0p", [H0, 3, P], BF16)
        m1r = sb("m1r", [H1, P])
        m1p = sb("m1p", [H1, 3, P], BF16)
        prob = [sb(f"prob{i}", [P, TH, P]) for i in range(NP)]
        rd0 = sb("rd0", [P, 2, H0 // 2, 1])
        rd1 = sb("rd1", [P, H1, 1])
        at0 = sb("at0", [P, H0, D0])
        at1 = sb("at1", [P, H1, D1])
        at0T = sb("at0T", [P, C, P])
        at1T = sb("at1T", [P, C, P])
        h0 = sb("h0", [P, D])
        h1 = sb("h1", [P, D])
        hb = sb("hb", [P, D])
        st0 = sb("st0", [P, 6])
        st1 = sb("st1", [P, 6])
        st2 = sb("st2", [P, 6])
        mv0 = sb("mv0", [P, 2])
        mv1 = sb("mv1", [P, 2])
        mv2 = sb("mv2", [P, 2])
        ve0 = sb("ve0", [P, 1])
        ve1 = sb("ve1", [P, 1])
        ve2 = sb("ve2", [P, 1])
        rs0 = sb("rs0", [P, 1])
        rs1 = sb("rs1", [P, 1])
        rs2 = sb("rs2", [P, 1])
        xg = sb("xg", [P, D])
        x1 = sb("x1", [P, D])
        x1b = sb("x1b", [P, 2, D])
        xn = sb("xn", [P, D])
        yn = sb("yn", [P, D])
        xnT = sb("xnT", [P, C, P])
        yT = sb("yT", [P, C, P])
        hT = sb("hT", [P, FC, P])
        ob = sb("ob", [P, 2, D])

        A = [ps(f"A{i}", [P, 512]) for i in range(2)]
        B = [ps(f"B{i}", [P, 512]) for i in range(2)]
        M = [ps(f"M{i}", [P, 512]) for i in range(2)]
        V = [ps(f"V{i}", [P, 512]) for i in range(2)]

        def scratch(name, shape):
            return nc.dram_tensor(name, shape, BF16, kind="Internal").ap()

        dq0 = [scratch(f"dq0_{i}", (3, D0, H0, P)) for i in range(2)]
        dk0 = [scratch(f"dk0_{i}", (3, D0, KV0, P)) for i in range(2)]
        dk1 = [scratch(f"dk1_{i}", (3, D1, H1, P)) for i in range(2)]
        dq1 = scratch("dq1", (3, D1, H1, P))
        dkb = scratch("dkb", (NB, P))

        names = """set_qk set_io set_mask set_w_kv set_w_attn set_w_mlp set_kbd set_dve set_absT set_pool sp_go mk_in mk_ok km_in
                   x_in xT_in cT_in xb_ok
                   qk_ps v_ps k1_ps qk_ev k1_ev v_ev sp0_hi sp0_r sp0_mid sp0_lo sp1_hi sp1_r sp1_mid sp1_lo
                   dq0_w dk0_w dk1_w k1_m
                   neg0T neg1T m0_split m1_split m0_in m1_in
                   ot0_ok ot1_ok ott0_ps ott1_ps rd0_ok rd1_ok at0_ok at1_ok
                   at0T_ps at1T_ps at0T_ok at1T_ok o0_ps o1_ps
                   h0_ok st0_ok mv0_ok ve0_ok rs0_ok xg_ok x1_ok x1b_ok st1_ok mv1_ok ve1_ok rs1_ok xn_ok
                   h1_ok hb_ok st2_ok mv2_ok ve2_ok rs2_ok yn_ok
                   xnT_ps xnT_ok yT_ps yT_ok q1_ps q1_ev q1_hi q1_r q1_mid q1_lo dq1_w
                   h_ps hT_ok y_ps out_ok st_even st_odd""".split()
        S = {n: sem("s_" + n) for n in names}
        q0_in, k0_in, k1_in, q1_in = (sem("s_" + n) for n in ("q0_in", "k0_in", "k1_in", "q1_in"))
        a_ps = [sem(f"s_a_ps{k}") for k in range(NT)]
        a_max = [sem(f"s_a_max{k}") for k in range(NT)]
        b_ps = [sem(f"s_b_ps{k}") for k in range(NT)]
        b_exp = [sem(f"s_b_exp{k}") for k in range(NT)]
        pv_ok = [sem(f"s_pv{k}") for k in range(NT)]

        class Has:
            def __init__(self, s):
                self.pre = 0 <= s + 1 < NB
                self.l0 = 0 <= s < NB
                self.q1 = 0 <= s - 1 < NB
                self.b1 = 0 <= s - 2 < NB
                self.mlp = 0 <= s - 3 < NB

        def steps(eng, step):
            for s in range(-1, 3):
                step(s, (s - 1) // 2, s % 2, Has(s))
            with eng.Fori(1, (NB - 2) // 2) as i:
                step(2 * i + 1, i, 1, Has(3))
                step(2 * i + 2, i, 0, Has(3))
            for s in range(NB - 1, NB + 3):
                step(s, (s - 1) // 2, s % 2, Has(s))

        def vslice(name):
            a, b = VEC[name]
            return vec[:, a:b]

        def stack(eng, done, src, dst, d, query):
            for part, reps, row in ((0, 3, 0), (1, 2, 3), (2, 1, 5)):
                if query:
                    eng.dma_start(dst[row * d:(row + reps) * d].rearrange("p h t -> p (h t)"),
                                  src[0:reps].rearrange("j d h t -> (j d) (h t)")).then_inc(done, 16)
                else:
                    one = src[part:part + 1].rearrange("j d h t -> j d (h t)")
                    eng.dma_start(dst[row * d:(row + reps) * d].rearrange("p h t -> p (h t)"),
                                  one.broadcast_to([reps, d, one.shape[2]])).then_inc(done, 16)

        def of(dram, b):
            return dram[b] if isinstance(b, int) else dram[bass.ds(b, 1)].squeeze(0)

        block = ctx.enter_context(nc.Block())

        @block.sync
        def _(sp):
            sp.sem_inc(S["st_even"], 16)
            sp.sem_inc(S["st_odd"], 16)
            for dst, src in ((xTs[:, 0], xT[0]), (w_qk[:], wqk), (cTs[:, 0], cT[0]), (col[:], cols), (kmr[:], kmask)):
                sp.dma_start(dst, src).then_inc(S["set_qk"], 16)
            sp.dma_start(maskq[:], mask.rearrange("b q k -> q b k")).then_inc(S["set_mask"], 16)
            sp.dma_start(mcur[:, 0], mask[0]).then_inc(S["set_io"], 16)
            sp.dma_start(kmu[:, 0], kmask[0].partition_broadcast(P)).then_inc(S["set_io"], 16)
            for dst, src in ((ident[:], eye), (vec[:], vecs.partition_broadcast(P)), (xs[:, 0], x[0])):
                sp.dma_start(dst, src).then_inc(S["set_io"], 16)
            for dst, src in ((w_k1, wk1), (w_v, wv)):
                sp.dma_start(dst[:], src).then_inc(S["set_w_kv"], 16)

            def load(b, slot):
                sp.dma_start(xTs[:, slot], of(xT, b)).then_inc(S["xT_in"], 16)
                sp.dma_start(cTs[:, slot], of(cT, b)).then_inc(S["cT_in"], 16)
                sp.dma_start(xs[:, slot], of(x, b)).then_inc(S["x_in"], 16)
                sp.dma_start(mcur[:, slot], of(mask, b)).then_inc(S["mk_in"], 16)
                sp.dma_start(kmu[:, slot], of(kmask, b).partition_broadcast(P)).then_inc(S["km_in"], 16)

            load(1, 1)
            sp.wait_ge(S["set_pool"], 8)
            sp.dma_start(dkb, kbias[:]).then_inc(S["set_kbd"], 16)
            sp.wait_ge(S["set_kbd"], 16)

            def step(s, stored, slot, has):
                other = 1 - slot

                def write_qk0():
                    sp.wait_ge(S["sp0_lo"], s + 2)
                    sp.dma_start(dq0[other].rearrange("j (c d) h t -> (d h) (j c) t", c=C),
                                 qkp[:, 0].rearrange("p j (c t) -> p (j c) t", c=C)).then_inc(S["dq0_w"], 16)
                    sp.dma_start(dk0[other].rearrange("j d h t -> (d h) j t"), qkp[0:KV0 * D0, 1, :, 0:P]).then_inc(S["dk0_w"], 16)

                if has.l0 and has.pre and has.q1:
                    sp.wait_ge(S["xb_ok"], s)
                    sp.sem_inc(S["sp_go"], 1)
                    sp.wait_ge(S["v_ps"], s)
                    sp.wait_ge(S["k1_ps"], s)
                    sp.wait_ge(S["mk_ok"], s)
                    sp.wait_ge(S["k1_ev"], s)
                    sp.sem_inc(S["sp_go"], 1)
                    load(s + 1, other)
                if has.b1 and has.q1:
                    sp.wait_ge(S["set_kbd"], 16)
                    sp.wait_ge(S["m1_split"], 4 * (s - 1))
                    for j in range(3):
                        sp.dma_start(QS1[M1R + j:M1R + j + 1], m1p[:, j]).then_inc(S["m1_in"], 16)
                if isinstance(s, int) and s == 0:
                    for dst, src in ((w_o, wo), (w_q1, wq1), (w_cp, wcp)):
                        sp.dma_start(dst[:], src).then_inc(S["set_w_attn"], 16)
                if isinstance(s, int) and s == 1:
                    for dst, src in ((w_fc, wfc), (w_pj, wpj)):
                        sp.dma_start(dst[:], src).then_inc(S["set_w_mlp"], 16)
                if has.q1:
                    sp.wait_ge(S["dk1_w"], 16 * s)
                    stack(sp, k1_in, dk1[other], KS1[other], D1, False)
                    sp.wait_ge(S["set_kbd"], 16)
                    sp.dma_start(KS1[other][R1:M1R], of(dkb, s - 1).unsqueeze(0).unsqueeze(0).broadcast_to([1, H1, P])).then_inc(S["k1_m"], 16)
                if has.pre and not has.q1:
                    write_qk0()
                if has.l0:
                    sp.wait_ge(S["set_kbd"], 16)
                    sp.wait_ge(S["m0_split"], 4 * (s + 1))
                    for j in range(3):
                        sp.dma_start(QS0[slot][R0 + j:R0 + j + 1], m0p[:, j]).then_inc(S["m0_in"], 16)
                if has.q1:
                    sp.wait_ge(S["q1_lo"], s)
                    sp.dma_start(dq1.rearrange("j (c d) h t -> (d h) (j c) t", c=C),
                                 q1p[:].rearrange("p j (c t) -> p (j c) t", c=C)).then_inc(S["dq1_w"], 16)
                if has.pre and has.q1:
                    write_qk0()
                if has.q1:
                    sp.wait_ge(S["dq1_w"], 16 * s)
                    if has.b1:
                        sp.wait_ge(b_ps[NT - 1], s - 1)
                    stack(sp, q1_in, dq1, QS1, D1, True)
                if has.pre:
                    if not has.l0:
                        sp.wait_ge(S["set_dve"], 2)
                    sp.wait_ge(S["dq0_w"], 16 * (s + 2))
                    stack(sp, q0_in, dq0[other], QS0[other], D0, True)
                if has.pre:
                    sp.wait_ge(S["dk0_w"], 16 * (s + 2))
                    stack(sp, k0_in, dk0[other], KS0[other], D0, False)
                if has.q1 and not has.l0:
                    sp.wait_ge(S["m1_split"], 4 * s)
                    for j in range(3):
                        sp.dma_start(QS1[M1R + j:M1R + j + 1], m1p[:, j]).then_inc(S["m1_in"], 16)
                if has.mlp:
                    sp.wait_ge(S["set_kbd"], 16)
                    sp.wait_ge(S["out_ok"], s - 2)
                    sp.dma_start(of(out, s - 3), ob[:, other]).then_inc(S["st_odd" if other else "st_even"], 16)
                if has.l0:
                    sp.wait_ge(S["sp1_lo"], s + 1)
                    sp.dma_start(dk1[slot].rearrange("j (c d) h t -> (d h) (j c) t", c=C),
                                 k1p[:].rearrange("p j (c t) -> p (j c) t", c=C)).then_inc(S["dk1_w"], 16)

            steps(sp, step)
            sp.wait_ge(S["st_even"], 16 * (NB // 2 + 1))
            sp.wait_ge(S["st_odd"], 16 * (NB // 2 + 1))

        @block.tensor
        def _(pe):
            mm = nc.tensor.matmul
            pe.wait_ge(S["set_qk"], 16 * 5)
            any_mask = None

            def load_flag():
                nonlocal any_mask
                pe.wait_ge(S["set_io"], 16 * 5)
                pe.wait_ge(S["set_dve"], 3)
                nc.tensor.transpose(V[0][0:1, 0:P], absm[:], ident[:]).then_inc(S["set_absT"], 1)
                pe.wait_ge(S["set_dve"], 4)
                any_mask = pe.value_load(flag[:].bitcast(I32), min_val=0, max_val=2 ** 31 - 1)

            def tile_a(s, slot, k, masked, bank_of):
                if k == T0:
                    pe.wait_ge(q1_in, 48 * s)
                    pe.wait_ge(k1_in, 48 * s)
                    pe.wait_ge(S["k1_m"], 16 * s)
                if bank_of is not None:
                    pe.wait_ge(a_max[bank_of], s + 1 if bank_of < T0 else s)
                for j in range(TH):
                    if k < T0:
                        last = mm(A[k % 2][:, j * P:(j + 1) * P], QS0[slot][0:R0, k * G0 + j], KS0[slot][0:R0, k],
                                  start=j == 0, stop=not masked, skip_group_check=True)
                    else:
                        h = (k - T0) * TH + j
                        last = mm(A[k % 2][:, j * P:(j + 1) * P], QS1[0:M1R, h], KS1[1 - slot][0:M1R, h],
                                  start=j == 0, stop=True, skip_group_check=True)
                if masked and k < T0:
                    last = mm(A[k % 2][:].rearrange("p (g k) -> p g k", g=G0), ident[:],
                              mcl[slot][:].unsqueeze(1).broadcast_to([P, G0, P]), start=False, stop=True, skip_group_check=True)
                last.then_inc(a_ps[k], 1)

            def tile_b(s, slot, k, masked, bank_of):
                if bank_of is not None:
                    pe.wait_ge(b_exp[bank_of], s + 1 if bank_of < T0 else s - 1)
                if k < T0:
                    last = mm(B[k % 2][:], KS0[slot][0:M0R, k], QS0[slot][0:M0R, k * G0:(k + 1) * G0],
                              start=True, stop=not masked, skip_group_check=True)
                    if masked:
                        for g in range(G0):
                            last = mm(B[k % 2][:, g * P:(g + 1) * P], mcl[slot][:], ident[:], start=False, stop=True,
                                      skip_group_check=True)
                else:
                    for j in range(TH):
                        h = (k - T0) * TH + j
                        last = mm(B[k % 2][:, j * P:(j + 1) * P], KS1[slot][0:M1E, h], QS1[0:M1E, h],
                                  start=j == 0, stop=True, skip_group_check=True)
                last.then_inc(b_ps[k], 1)

            def tile_pv(s, slot, k):
                pe.wait_ge(b_exp[k], s + 1 if k < T0 else s - 1)
                if k < T0:
                    q = k % TH * W
                    last = mm(V[k // TH][q:q + W, :], V0[:, k], prob[k % NP][:].rearrange("p h t -> p (h t)"),
                              start=True, stop=True, skip_group_check=True)
                else:
                    for j in range(TH):
                        h = (k - T0) * TH + j
                        last = mm(V[0][j * W:(j + 1) * W, (k - T0) * P:(k - T0 + 1) * P], V1[slot][:, h], prob[k % NP][:, j],
                                  start=True, stop=True, skip_group_check=True)
                last.then_inc(pv_ok[k], 1)

            def flip(dst, src, done):
                for c in range(C):
                    last = nc.tensor.transpose(dst[:, c * P:(c + 1) * P], src[:, c * P:(c + 1) * P], ident[:])
                last.then_inc(done, 1)

            def tokens_out(dst, lhs, w):
                chunks = w.shape[1]
                for c in range(chunks):
                    last = mm(dst, lhs[:, c], w[:, c], start=c == 0, stop=c == chunks - 1, skip_group_check=True)
                return last

            def dims_out(dst, w, rhs, m):
                for c in range(C):
                    last = mm(dst, w[:, c, m * P:(m + 1) * P], rhs[:, c], start=m == 0 and c == 0, stop=c == C - 1, skip_group_check=True)
                return last

            def turn(dst, src, done):
                for t in range(TH):
                    last = nc.tensor.transpose(dst[:, t * P:(t + 1) * P], src[:, t * P:(t + 1) * P], ident[:])
                last.then_inc(done, 1)

            def stay_awake(n):
                for _ in range(n):
                    mm(M[0][:, 0:P], ident[:], ident[:], start=True, stop=True, skip_group_check=True)

            def step(s, stored, slot, has):
                other = 1 - slot

                if isinstance(s, int) and s == 0:
                    load_flag()
                if isinstance(s, int) and s == 1:
                    pe.wait_ge(S["set_w_attn"], 16 * 3)
                    pe.wait_ge(S["set_pool"], 7)
                if isinstance(s, int) and s == 2:
                    pe.wait_ge(S["set_w_mlp"], 16 * 2)

                def mlp_up(q):
                    if has.mlp:
                        hidden = B if has.q1 else A
                        if q == 0:
                            pe.wait_ge(S["yT_ok"], s - 2)
                        for r in range(2 * q, 2 * q + 2):
                            m = r % TH
                            for c in range(C):
                                last = mm(hidden[r // TH][:, m * P:(m + 1) * P], w_fc[:, c, r * P:(r + 1) * P], yT[:, c],
                                          start=m == 0 and c == 0, stop=c == C - 1, skip_group_check=True)
                        if q % 2 == 1:
                            last.then_inc(S["h_ps"], 1)

                def mlp_down(a):
                    if has.mlp:
                        pe.wait_ge(S["hT_ok"], 2 * s - 5 + a)
                        if a == 0 and has.q1:
                            if has.l0:
                                pe.wait_ge(S["k1_ev"], s + 1)
                            else:
                                pe.wait_ge(S["xnT_ok"], s)
                        elif a == 0 and not has.b1:
                            pe.wait_ge(S["out_ok"], s - 3)
                        for m in range(a * TH, (a + 1) * TH):
                            last = mm((M[1] if has.q1 else V[1])[:, 0:D], hT[:, m], w_pj[:, m], start=m == 0, stop=m == FC - 1, skip_group_check=True)
                        if a == 1:
                            last.then_inc(S["y_ps"], 1)

                def turn0(a, n):
                    pe.wait_ge(S["ot0_ok"], 2 * n - 1 + a)
                    turn(V[a], ot0[:, a], S["ott0_ps"])

                def at0_flip():
                    pe.wait_ge(S["at0_ok"], 2 * s)
                    if has.mlp:
                        pe.wait_ge(S["h1_ok"], s - 2)
                    elif has.b1:
                        pe.wait_ge(S["k1_ev"], s)
                    else:
                        pe.wait_ge(S["qk_ev"], s + 1)
                    flip(M[1], at0[:].rearrange("p h d -> p (h d)"), S["at0T_ps"])

                def out0():
                    pe.wait_ge(S["at0T_ok"], s)
                    if has.mlp and has.l0:
                        pe.wait_ge(S["yT_ok"], s - 2)
                    elif has.l0:
                        pe.wait_ge(S["v_ev"], s)
                    tokens_out(M[0][:, 0:D], at0T, w_o).then_inc(S["o0_ps"], 1)

                def project_qk():
                    if has.l0:
                        pe.wait_ge(S["xT_in"], 16 * (s + 1))
                        pe.wait_ge(S["cT_in"], 16 * (s + 1))
                    if isinstance(s, int) and s == 0:
                        pe.wait_ge(S["k1_ev"], s + 1)
                    for m in range(C):
                        dims_out(M[1][:, m * P:(m + 1) * P], w_qk, xTs[:, other], m)
                    for c in range(C):
                        last = mm(M[1][:, D:D + P], w_qk[:, c, D:D + P], cTs[:, other, c], start=False, stop=c == C - 1,
                                  skip_group_check=True)
                    last.then_inc(S["qk_ps"], 1)

                def project_kv():
                    if isinstance(s, int) and s == 0:
                        pe.wait_ge(S["set_w_kv"], 16 * 2)
                        pe.wait_ge(S["qk_ev"], s + 1)
                    else:
                        pe.wait_ge(S["xnT_ok"], s)
                    for m in range(C):
                        last = dims_out(M[1][:, m * P:(m + 1) * P], w_k1, cTs[:, slot], m)
                    last.then_inc(S["k1_ps"], 1)
                    if not (isinstance(s, int) and s == 0):
                        pe.wait_ge(S["q1_ev"], s)
                    tokens_out(M[0][:, 0:KV0 * D0 + D], cTs[:, slot], w_v).then_inc(S["v_ps"], 1)

                def xn_flip():
                    pe.wait_ge(S["xn_ok"], s)
                    if has.pre:
                        pe.wait_ge(S["qk_ev"], s + 2)
                    flip(M[1], xn[:], S["xnT_ps"])

                def y_flip(n):
                    pe.wait_ge(S["yn_ok"], n)
                    flip(M[0], yn[:], S["yT_ps"])

                def turn1():
                    pe.wait_ge(S["ot1_ok"], s - 1)
                    turn(V[0], ot1[:], S["ott1_ps"])

                def at1_flip():
                    pe.wait_ge(S["at1_ok"], s - 1)
                    if has.l0:
                        pe.wait_ge(S["v_ev"], s + 1)
                    elif has.q1:
                        pe.wait_ge(S["q1_ev"], s)
                    else:
                        pe.wait_ge(S["yT_ok"], s - 2)
                    flip(M[0], at1[:].rearrange("p h d -> p (h d)"), S["at1T_ps"])

                def out1():
                    pe.wait_ge(S["at1T_ok"], s - 1)
                    if not has.q1:
                        pe.wait_ge(S["h1_ok"], s - 2)
                    elif has.mlp:
                        pe.wait_ge(S["out_ok"], s - 2)
                    else:
                        pe.wait_ge(S["k1_ev"], s + 1)
                    tokens_out(M[1][:, 0:D], at1T, w_cp).then_inc(S["o1_ps"], 1)

                def attention1():
                    pe.wait_ge(S["m1_in"], 48 * (s - 1))
                    if has.q1:
                        pe.wait_ge(S["hT_ok"], 2 * s - 4)
                    tile_b(s, slot, T0, False, None)
                    tile_b(s, slot, T0 + 1, False, None)
                    if has.q1:
                        mlp_down(0)
                    tile_b(s, slot, T0 + 2, False, T0)
                    tile_pv(s, slot, T0)
                    tile_b(s, slot, T0 + 3, False, T0 + 1)
                    for k in range(T0 + 1, NT):
                        tile_pv(s, slot, k)

                def project_q1():
                    pe.wait_ge(S["xnT_ok"], s)
                    pe.wait_ge(S["h0_ok"], s)
                    for m in range(C):
                        last = dims_out(M[0][:, m * P:(m + 1) * P], w_q1, xnT, m)
                    last.then_inc(S["q1_ps"], 1)

                def negated(src, dst, last_max, n, done):
                    pe.wait_ge(last_max, n)
                    nc.tensor.transpose(dst[:, 0:P], src[:], ident[:]).then_inc(done, 1)

                def tiles(masked):
                    max0 = lambda k: tile_a(s, slot, k, masked, k - 2 if k >= 2 else None)
                    max1 = lambda k: tile_a(s, slot, k, False, k - 2 if k >= T0 + 2 else None) if has.q1 else None
                    exp0 = lambda k: tile_b(s, slot, k, masked, k - 2 if k >= 2 else None)
                    exp1 = lambda k: tile_b(s, slot, k, False, k - 2 if k >= T0 + 2 else None) if has.b1 else None
                    pv0 = lambda k: tile_pv(s, slot, k)
                    pv1 = lambda k: tile_pv(s, slot, k) if has.b1 else None

                    pe.wait_ge(q0_in, 48 * (s + 1))
                    pe.wait_ge(k0_in, 48 * (s + 1))
                    pe.wait_ge(S["mk_ok"], s + 1)
                    if has.b1:
                        pe.wait_ge(a_max[NT - 2], s - 1)
                    max0(0)
                    if has.mlp:
                        y_flip(s - 2)
                    if has.q1:
                        turn0(1, s)
                    if has.b1:
                        pe.wait_ge(a_max[NT - 1], s - 1)
                    max0(1)
                    if has.b1:
                        pe.wait_ge(S["at0_ok"], 2 * s - 1)
                        negated(negm1, V[0], a_max[NT - 1], s - 1, S["neg1T"])
                    mlp_up(0)
                    if has.q1:
                        at0_flip()
                    mlp_up(1)
                    if has.q1:
                        out0()
                    max0(2)
                    mlp_up(2)
                    mlp_up(3)
                    max0(3)
                    if has.pre and has.q1:
                        project_qk()
                    max0(4)
                    if has.b1:
                        pe.wait_ge(S["m1_in"], 48 * (s - 1))
                        if has.mlp:
                            pe.wait_ge(S["hT_ok"], 2 * s - 4)
                    exp1(T0)
                    exp1(T0 + 1)
                    max0(5)
                    exp1(T0 + 2)
                    pv1(T0)
                    max0(6)
                    exp1(T0 + 3)
                    pv1(T0 + 1)
                    max0(7)
                    if has.q1:
                        xn_flip()
                    pv1(T0 + 2)
                    negated(negm0, V[1], a_max[T0 - 1], s + 1, S["neg0T"])
                    if has.q1:
                        project_q1()
                    pv1(T0 + 3)

                    if has.q1:
                        project_kv()
                    mlp_down(0)
                    if has.b1:
                        turn1()

                    if isinstance(s, int) and s == 0:
                        stay_awake(10)
                    pe.wait_ge(S["m0_in"], 48 * (s + 1))
                    exp0(0)
                    exp0(1)
                    mlp_down(1)
                    if has.b1:
                        at1_flip()
                    exp0(2)
                    pe.wait_ge(S["v_ev"], s + 1)
                    pv0(0)
                    exp0(3)
                    pv0(1)
                    exp0(4)
                    pv0(2)
                    if has.b1:
                        out1()
                    exp0(5)
                    pv0(3)
                    max1(T0)
                    exp0(6)
                    pv0(4)
                    max1(T0 + 1)
                    exp0(7)
                    pv0(5)
                    turn0(0, s + 1)
                    max1(T0 + 2)
                    pv0(6)
                    pv0(7)
                    max1(T0 + 3)

                def last_output():
                    turn0(1, s)
                    pe.wait_ge(S["at0_ok"], 2 * s - 1)
                    negated(negm1, V[0], a_max[NT - 1], s - 1, S["neg1T"])
                    at0_flip()
                    out0()
                    pe.wait_ge(S["h0_ok"], s)
                    y_flip(s - 2)
                    for q in range(3):
                        mlp_up(q)
                    xn_flip()
                    mlp_up(3)
                    project_q1()
                    attention1()
                    mlp_down(1)
                    stay_awake(5)
                    tile_a(s, slot, T0, False, None)
                    tile_a(s, slot, T0 + 1, False, None)
                    turn1()
                    tile_a(s, slot, T0 + 2, False, T0)
                    tile_a(s, slot, T0 + 3, False, T0 + 1)
                    at1_flip()
                    negated(negm1, V[1], a_max[NT - 1], s, S["neg1T"])
                    out1()

                def last_attention():
                    pe.wait_ge(S["at1T_ok"], s - 2)
                    stay_awake(10)
                    y_flip(s - 2)
                    attention1()
                    mlp_up(0)
                    turn1()
                    mlp_up(1)
                    at1_flip()
                    mlp_up(2)
                    out1()
                    mlp_up(3)
                    mlp_down(0)
                    y_flip(s - 1)
                    mlp_down(1)

                def last_mlp():
                    for q in range(4):
                        mlp_up(q)
                    mlp_down(0)
                    mlp_down(1)

                if isinstance(s, int) and s == 0:
                    project_kv()
                    project_qk()
                    pe.wait_ge(S["v_ev"], s + 1)
                    stay_awake(6)
                if has.l0:
                    with pe.If(any_mask > 0):
                        tiles(True)
                    with pe.Else():
                        tiles(False)
                    pe.nop()
                elif has.pre:
                    project_qk()
                elif has.q1:
                    last_output()
                elif has.b1:
                    last_attention()
                else:
                    last_mlp()

            steps(pe, step)

        @block.vector
        def _(dve):
            v = nc.vector
            v.memset(qk32[:, 1, P:2 * P], 0.0)
            v.memset(negm0[:], 0.0)
            v.memset(negm1[:], 0.0)
            v.memset(V0[:], 0.0)
            for i in range(2):
                v.memset(KS0[i][32:2 * 32], 1.0)
                v.memset(V1[i][:], 0.0).then_inc(S["set_dve"], 1)
            dve.wait_ge(S["set_dve"], 2)
            v.memset(V0[:, :, D0:D0 + 1], 1.0)
            for i in range(2):
                v.memset(V1[i][:, :, D1:D1 + 1], 1.0)
            dve.wait_ge(S["set_mask"], 16)
            v.tensor_reduce(absm[:], maskq[:].rearrange("p b k -> p (b k)"), AX.X, ALU.max, apply_absolute_value=True)\
                .then_inc(S["set_dve"], 1)

            def stats(x_, ready, n, st, done):
                dve.wait_ge(ready, n)
                v.bn_stats(st[:], x_).then_inc(done, 1)

            def mean_var(n, st, mv, ve, eps, st_ok, mv_ok, ve_ok):
                dve.wait_ge(S["set_dve"], 2)
                dve.wait_ge(st_ok, n)
                v.bn_aggr(mv[:], st[:]).then_inc(mv_ok, 1)
                dve.wait_ge(mv_ok, n)
                v.tensor_scalar(ve[:], mv[:, 1:2], eps, None, ALU.add).then_inc(ve_ok, 1)

            def split_max(src, ready, n, mp, mr, done):
                dve.wait_ge(ready, n)
                v.tensor_copy(mp[:, 0], src).then_inc(done, 1)
                dve.wait_ge(done, 4 * n - 3)
                v.tensor_tensor(mr[:], src, mp[:, 0], ALU.subtract).then_inc(done, 1)
                dve.wait_ge(done, 4 * n - 2)
                v.tensor_copy(mp[:, 1], mr[:]).then_inc(done, 1)
                dve.wait_ge(done, 4 * n - 1)
                v.tensor_tensor(mp[:, 2], mr[:], mp[:, 1], ALU.subtract).then_inc(done, 1)

            def step(s, stored, slot, has):
                other = 1 - slot

                def top(k):
                    if has.l0 if k < T0 else has.q1:
                        dve.wait_ge(a_ps[k], s + 1 if k < T0 else s)
                        dst = negm0[:, k * TH:(k + 1) * TH] if k < T0 else negm1[:, (k - T0) * TH:(k - T0 + 1) * TH]
                        v.tensor_reduce(dst, A[k % 2][:].rearrange("p (g k) -> p g k", g=TH), AX.X, ALU.max, negate=True)\
                            .then_inc(a_max[k], 1)

                def join_mlp():
                    dve.wait_ge(S["y_ps"], s - 2)
                    dve.wait_ge(S["hb_ok"], s - 2)
                    dve.wait_ge(S["st_odd" if other else "st_even"], 16 * stored)
                    v.tensor_tensor(ob[:, other], (M[1] if has.q1 else V[1])[:, 0:D], hb[:], ALU.add).then_inc(S["out_ok"], 1)

                def divide0(a, n):
                    pv = V[a][:].rearrange("p (g j w) -> p j g w", j=TH, w=W)
                    r = rd0[:, a].rearrange("p (j g) o -> p j g o", g=G0)
                    dve.wait_ge(S["ott0_ps"], 2 * n - 1 + a)
                    v.reciprocal(r, pv[:, :, :, D0:D0 + 1]).then_inc(S["rd0_ok"], 1)
                    dve.wait_ge(S["rd0_ok"], 2 * n - 1 + a)
                    v.tensor_tensor(at0[:, a * H0 // 2:(a + 1) * H0 // 2].rearrange("p (j g) d -> p j g d", g=G0),
                                    pv[:, :, :, 0:D0], r.broadcast_to([P, TH, G0, D0]), ALU.mult).then_inc(S["at0_ok"], 1)

                def residual0():
                    dve.wait_ge(S["o0_ps"], s)
                    dve.wait_ge(S["xb_ok"], s)
                    v.tensor_tensor(h0[:], M[0][:, 0:D], xb[:, other], ALU.add).then_inc(S["h0_ok"], 1)
                    stats(h0[:], S["h0_ok"], s, st0, S["st0_ok"])

                def centre0():
                    mean_var(s, st0, mv0, ve0, EPS0, S["st0_ok"], S["mv0_ok"], S["ve0_ok"])
                    v.scalar_tensor_tensor(xg[:], h0[:], mv0[:, 0:1], vslice("gamma"), ALU.subtract, ALU.mult).then_inc(S["xg_ok"], 1)

                def norm0():
                    dve.wait_ge(S["rs0_ok"], s)
                    dve.wait_ge(S["xg_ok"], s)
                    v.scalar_tensor_tensor(x1[:], xg[:], rs0[:], vslice("beta"), ALU.mult, ALU.add).then_inc(S["x1_ok"], 1)
                    stats(x1[:], S["x1_ok"], s, st1, S["st1_ok"])

                def mean1():
                    mean_var(s, st1, mv1, ve1, EPS1, S["st1_ok"], S["mv1_ok"], S["ve1_ok"])

                def norm1():
                    dve.wait_ge(S["rs1_ok"], s)
                    v.tensor_scalar(xn[:], x1[:], mv1[:, 0:1], rs1[:], ALU.subtract, ALU.mult).then_inc(S["xn_ok"], 1)

                def divide1():
                    pv1 = V[0][:].rearrange("p (h w) -> p h w", w=W)
                    dve.wait_ge(S["ott1_ps"], s - 1)
                    v.reciprocal(rd1[:], pv1[:, :, D1:D1 + 1]).then_inc(S["rd1_ok"], 1)
                    dve.wait_ge(S["rd1_ok"], s - 1)
                    v.tensor_tensor(at1[:], pv1[:, :, 0:D1], rd1[:].broadcast_to([P, H1, D1]), ALU.mult).then_inc(S["at1_ok"], 1)

                def residual1():
                    dve.wait_ge(S["o1_ps"], s - 1)
                    dve.wait_ge(S["x1b_ok"], s - 1)
                    if has.mlp and not has.l0:
                        dve.wait_ge(S["hb_ok"], s - 2)
                    v.tensor_tensor(h1[:], M[1][:, 0:D], x1b[:, slot], ALU.add).then_inc(S["h1_ok"], 1)
                    stats(h1[:], S["h1_ok"], s - 1, st2, S["st2_ok"])

                def mean2():
                    mean_var(s - 1, st2, mv2, ve2, EPS1, S["st2_ok"], S["mv2_ok"], S["ve2_ok"])

                def norm2():
                    dve.wait_ge(S["rs2_ok"], s - 1)
                    v.tensor_scalar(yn[:], h1[:], mv2[:, 0:1], rs2[:], ALU.subtract, ALU.mult).then_inc(S["yn_ok"], 1)

                def q1_rest():
                    dve.wait_ge(S["q1_hi"], s)
                    v.tensor_tensor(q1r[:], q32[:], q1p[:, 0], ALU.subtract).then_inc(S["q1_r"], 1)

                def q1_last():
                    dve.wait_ge(S["q1_mid"], s)
                    v.tensor_tensor(q1p[:, 2], q1r[:], q1p[:, 1], ALU.subtract).then_inc(S["q1_lo"], 1)

                def k1_out():
                    dve.wait_ge(S["k1_ps"], s + 1)
                    if isinstance(s, int) and s == 0:
                        dve.wait_ge(S["set_io"], 16 * 5)
                    else:
                        dve.wait_ge(S["km_in"], 16 * s)
                    if not (isinstance(s, int) and s == 0):
                        dve.wait_ge(S["sp1_lo"], s)
                    for c in range(C):
                        last = v.scalar_tensor_tensor(k32[:, c * P:(c + 1) * P], M[1][:, c * P:(c + 1) * P],
                                                      col[:, COL["k1"] + c:COL["k1"] + c + 1], kmu[:, slot], ALU.add, ALU.mult)
                    last.then_inc(S["k1_ev"], 1)

                def v_out():
                    dve.wait_ge(S["v_ps"], s + 1)
                    if isinstance(s, int) and s == 0:
                        dve.wait_ge(S["set_io"], 16 * 5)
                    v.tensor_tensor(V0[:, :, 0:D0], M[0][:, 0:KV0 * D0].rearrange("p (h d) -> p h d", d=D0),
                                    vslice("v0").rearrange("p (h d) -> p h d", d=D0), ALU.add)
                    v.tensor_tensor(V1[slot][:, :, 0:D1], M[0][:, KV0 * D0:KV0 * D0 + D].rearrange("p (h d) -> p h d", d=D1),
                                    vslice("v1").rearrange("p (h d) -> p h d", d=D1), ALU.add).then_inc(S["v_ev"], 1)

                if has.l0 or has.pre:
                    if isinstance(s, int) and s == 0:
                        dve.wait_ge(S["set_absT"], 1)
                        v.tensor_reduce(flag[:], V[0][0:1, 0:P], AX.X, ALU.max).then_inc(S["set_dve"], 1)
                        k1_out()
                        v_out()
                    if has.q1:
                        divide0(1, s)
                    top(0)
                    top(1)
                    if has.b1:
                        split_max(V[0][0:H1, 0:P], S["neg1T"], s - 1, m1p, m1r, S["m1_split"])
                    if has.q1:
                        residual0()
                    top(2)
                    if has.q1:
                        centre0()
                    top(3)
                    if has.q1:
                        norm0()
                    top(4)
                    if has.q1:
                        mean1()
                    top(5)
                    if has.q1:
                        norm1()
                    top(6)
                    top(7)
                    if has.l0:
                        split_max(V[1][0:H0, 0:P], S["neg0T"], s + 1, m0p, m0r, S["m0_split"])
                    if has.q1:
                        q1_rest()
                    if has.q1:
                        if has.l0:
                            k1_out()
                        q1_last()
                        if has.l0:
                            v_out()
                    if has.pre:
                        if has.l0:
                            dve.wait_ge(S["mk_in"], 16 * (s + 1))
                        else:
                            dve.wait_ge(S["set_io"], 16 * 5)
                        v.tensor_scalar(mcl[other][:], mcur[:, other], LOWEST, None, ALU.max).then_inc(S["mk_ok"], 1)
                    if has.b1:
                        divide1()
                    if has.mlp:
                        join_mlp()
                    if has.b1:
                        residual1()
                    top(T0)
                    if has.b1:
                        mean2()
                    top(T0 + 1)
                    if has.b1:
                        norm2()
                    top(T0 + 2)
                    if has.l0:
                        divide0(0, s + 1)
                    top(T0 + 3)
                elif has.q1:
                    divide0(1, s)
                    split_max(V[0][0:H1, 0:P], S["neg1T"], s - 1, m1p, m1r, S["m1_split"])
                    residual0()
                    centre0()
                    norm0()
                    mean1()
                    norm1()
                    q1_rest()
                    q1_last()
                    top(T0)
                    top(T0 + 1)
                    divide1()
                    top(T0 + 2)
                    top(T0 + 3)
                    join_mlp()
                    split_max(V[1][0:H1, 0:P], S["neg1T"], s, m1p, m1r, S["m1_split"])
                    residual1()
                    mean2()
                    norm2()
                elif has.b1:
                    divide1()
                    residual1()
                    mean2()
                    norm2()
                    join_mlp()
                else:
                    join_mlp()

            steps(dve, step)

        @block.scalar
        def _(act):
            a = nc.scalar.activation
            act.wait_ge(S["set_pool"], 1)
            a(warm[:], half[:], ACT.Exp)
            act.wait_ge(S["set_qk"], 16 * 5)
            act.wait_ge(S["set_pool"], 6)

            def step(s, stored, slot, has):
                def exp(k):
                    if has.l0 if k < T0 else has.b1:
                        act.wait_ge(b_ps[k], s + 1 if k < T0 else s - 1)
                        if k >= T0:
                            if has.q1:
                                act.wait_ge(pv_ok[k - NP], s)
                        elif k >= NP:
                            act.wait_ge(pv_ok[k - NP], s + 1)
                        elif has.b1:
                            act.wait_ge(pv_ok[k + T0], s - 1)
                        a(prob[k % NP][:].rearrange("p h t -> p (h t)"), B[k % 2][:], ACT.Exp).then_inc(b_exp[k], 1)

                def xn_turned():
                    act.wait_ge(S["xnT_ps"], s)
                    for c in range(C):
                        last = a(xnT[:, c], M[1][:, c * P:(c + 1) * P], ACT.Identity, bias=col[:, COL["b1"] + c:COL["b1"] + c + 1],
                                 scale=col[:, COL["w1"] + c:COL["w1"] + c + 1])
                    last.then_inc(S["xnT_ok"], 1)

                def q1_parts():
                    act.wait_ge(S["q1_ps"], s)
                    for c in range(C):
                        last = a(q32[:, c * P:(c + 1) * P], M[0][:, c * P:(c + 1) * P], ACT.Identity, bias=sbias[:, 2 + c:3 + c], scale=S1)
                    last.then_inc(S["q1_ev"], 1)
                    act.wait_ge(S["q1_ev"], s)
                    if has.b1:
                        act.wait_ge(S["dq1_w"], 16 * (s - 1))
                    a(q1p[:, 0], q32[:], ACT.Copy).then_inc(S["q1_hi"], 1)

                def qk_hi():
                    act.wait_ge(S["qk_ev"], s + 2)
                    if has.l0:
                        act.wait_ge(S["dq0_w"], 16 * (s + 1))
                        act.wait_ge(S["dk0_w"], 16 * (s + 1))
                    a(qkp[:, :, 0], qk32[:], ACT.Copy).then_inc(S["sp0_hi"], 1)

                def qk_mid():
                    act.wait_ge(S["sp0_r"], s + 2)
                    a(qkp[:, :, 1], qkr[:], ACT.Copy).then_inc(S["sp0_mid"], 1)

                def q1_mid():
                    act.wait_ge(S["q1_r"], s)
                    a(q1p[:, 1], q1r[:], ACT.Copy).then_inc(S["q1_mid"], 1)

                def sums0(half_):
                    act.wait_ge(pv_ok[(half_ + 1) * TH - 1], s + 1)
                    a(ot0[:, half_], V[half_][:], ACT.Copy).then_inc(S["ot0_ok"], 1)

                def y_turned():
                    act.wait_ge(S["yT_ps"], s - 2)
                    for c in range(C):
                        last = a(yT[:, c], M[0][:, c * P:(c + 1) * P], ACT.Identity, bias=col[:, COL["b2"] + c:COL["b2"] + c + 1],
                                 scale=col[:, COL["w2"] + c:COL["w2"] + c + 1])
                    last.then_inc(S["yT_ok"], 1)

                def at0_turned():
                    act.wait_ge(S["at0T_ps"], s)
                    a(at0T[:].rearrange("p c t -> p (c t)"), M[1][:, 0:D], ACT.Copy).then_inc(S["at0T_ok"], 1)

                def gelu(half_):
                    act.wait_ge(S["h_ps"], 2 * s - 5 + half_)
                    for m in range(half_ * TH, (half_ + 1) * TH):
                        last = a(hT[:, m], (B if has.q1 else A)[half_][:, (m % TH) * P:(m % TH + 1) * P], ACT.Gelu_apprx_tanh,
                                 bias=col[:, COL["fc"] + m:COL["fc"] + m + 1])
                    last.then_inc(S["hT_ok"], 1)

                def sums1():
                    act.wait_ge(pv_ok[NT - 1], s - 1)
                    a(ot1[:], V[0][:], ACT.Copy).then_inc(S["ot1_ok"], 1)

                def at1_turned():
                    act.wait_ge(S["at1T_ps"], s - 1)
                    a(at1T[:].rearrange("p c t -> p (c t)"), M[0][:, 0:D], ACT.Copy).then_inc(S["at1T_ok"], 1)

                if has.l0 or has.pre:
                    if has.mlp:
                        y_turned()
                    if has.q1:
                        at0_turned()
                    if has.mlp:
                        gelu(0)
                        gelu(1)
                    exp(T0)
                    exp(T0 + 1)
                    if has.pre:
                        act.wait_ge(S["qk_ps"], s + 2)
                        if has.l0:
                            act.wait_ge(S["sp0_lo"], s + 1)
                        else:
                            act.wait_ge(S["set_dve"], 2)
                        for c in range(C):
                            a(qk32[:, 0, c * P:(c + 1) * P], M[1][:, c * P:(c + 1) * P], ACT.Identity, bias=sbias[:, c:c + 1], scale=S0)
                        a(qk32[:, 1, 0:P], M[1][:, D:D + P], ACT.Identity, bias=col[:, COL["k0"]:COL["k0"] + 1]).then_inc(S["qk_ev"], 1)
                        if not has.mlp:
                            qk_hi()
                    exp(T0 + 2)
                    if has.q1:
                        xn_turned()
                    exp(T0 + 3)
                    if has.pre:
                        if has.mlp:
                            qk_hi()
                        else:
                            qk_mid()
                    if has.q1:
                        q1_parts()
                    if has.pre and has.mlp:
                        qk_mid()
                    if has.b1:
                        sums1()
                    if has.q1:
                        q1_mid()
                    if has.l0:
                        act.wait_ge(S["k1_ev"], s + 1)
                        if not (isinstance(s, int) and s == 0):
                            act.wait_ge(S["dk1_w"], 16 * s)
                        a(k1p[:, 0], k32[:], ACT.Copy).then_inc(S["sp1_hi"], 1)
                    exp(0)
                    exp(1)
                    if has.b1:
                        at1_turned()
                    if has.l0:
                        act.wait_ge(S["sp1_r"], s + 1)
                        a(k1p[:, 1], k1r[:], ACT.Copy).then_inc(S["sp1_mid"], 1)
                    for k in range(2, 6):
                        exp(k)
                    if has.l0:
                        sums0(0)
                    exp(6)
                    exp(7)
                    if has.l0:
                        sums0(1)
                elif has.q1:
                    at0_turned()
                    y_turned()
                    gelu(0)
                    xn_turned()
                    gelu(1)
                    q1_parts()
                    q1_mid()
                    for k in range(T0, NT):
                        exp(k)
                    sums1()
                    at1_turned()
                elif has.b1:
                    y_turned()
                    for k in range(T0, NT):
                        exp(k)
                    sums1()
                    at1_turned()
                    gelu(0)
                    gelu(1)
                else:
                    y_turned()
                    gelu(0)
                    gelu(1)

            steps(act, step)

        @block.gpsimd
        def _(pool):
            g = nc.gpsimd
            g.memset(half[:], -0.5).then_inc(S["set_pool"], 1)
            for n, rows_ in enumerate((QS1, KS1[0], KS1[1])):
                pool.wait_ge(S["set_pool"], n + 1)
                g.memset(rows_[R1:P], 1.0).then_inc(S["set_pool"], 1)
            pool.wait_ge(S["set_pool"], 4)
            pool.wait_ge(S["set_qk"], 16 * 5)
            g.tensor_scalar(sbias[:, 0:2], col[:, COL["q0"]:COL["q0"] + 2], S0, None, ALU.mult).then_inc(S["set_pool"], 1)
            pool.wait_ge(S["set_pool"], 5)
            g.tensor_scalar(sbias[:, 2:4], col[:, COL["q1"]:COL["q1"] + 2], S1, None, ALU.mult).then_inc(S["set_pool"], 1)
            pool.wait_ge(S["set_pool"], 6)
            g.tensor_copy(kmf[:], kmr[:]).then_inc(S["set_pool"], 1)
            pool.wait_ge(S["set_pool"], 7)
            g.tensor_scalar(kbias[:], kmf[:], 1.0, MASKED, ALU.subtract, ALU.mult).then_inc(S["set_pool"], 1)

            def inverse_root(ve, rs, n, stats_done, t_out):
                pool.wait_ge(stats_done, n)
                g.tensor_tensor(rs[:], ve[:], half[:], ALU.pow).then_inc(S[t_out], 1)

            def step(s, stored, slot, has):
                other = 1 - slot
                if has.q1:
                    inverse_root(ve0, rs0, s, S["ve0_ok"], "rs0_ok")
                if has.q1:
                    inverse_root(ve1, rs1, s, S["ve1_ok"], "rs1_ok")
                if has.pre:
                    pool.wait_ge(S["sp0_hi"], s + 2)
                    g.tensor_tensor(qkr[:], qk32[:], qkp[:, :, 0], ALU.subtract).then_inc(S["sp0_r"], 1)
                if has.pre:
                    pool.wait_ge(S["sp0_mid"], s + 2)
                    g.tensor_tensor(qkp[:, :, 2], qkr[:], qkp[:, :, 1], ALU.subtract).then_inc(S["sp0_lo"], 1)
                if has.q1:
                    g.tensor_tensor(x1b[:, other], x1[:], vslice("cp"), ALU.add).then_inc(S["x1b_ok"], 1)
                if has.l0:
                    if isinstance(s, int) and s == 0:
                        pool.wait_ge(S["set_io"], 16 * 5)
                    else:
                        pool.wait_ge(S["x_in"], 16 * s)
                    g.tensor_tensor(xb[:, slot], xs[:, slot], vslice("bo"), ALU.add).then_inc(S["xb_ok"], 1)
                    pool.wait_ge(S["sp1_hi"], s + 1)
                    g.tensor_tensor(k1r[:], k32[:], k1p[:, 0], ALU.subtract).then_inc(S["sp1_r"], 1)
                    pool.wait_ge(S["sp1_mid"], s + 1)
                    g.tensor_tensor(k1p[:, 2], k1r[:], k1p[:, 1], ALU.subtract).then_inc(S["sp1_lo"], 1)
                if has.b1:
                    inverse_root(ve2, rs2, s - 1, S["ve2_ok"], "rs2_ok")
                    if has.mlp and not has.l0:
                        pool.wait_ge(S["out_ok"], s - 2)
                    g.tensor_tensor(hb[:], h1[:], vslice("pb"), ALU.add).then_inc(S["hb_ok"], 1)

            steps(pool, step)


_OUT = (NB, P, D)


def kernel(**inputs):
    import numpy as np
    import concourse.bacc as bacc
    from concourse import mybir as mb
    from concourse.bass_utils import run_bass_kernel_spmd as run

    g = {k: np.asarray(v) for k, v in inputs.items()}

    def rows(w):
        return w.reshape(-1, P, w.shape[1]).transpose(1, 0, 2)

    def heads_inner(w, h, d):
        return w.reshape(w.shape[:-1] + (h, d)).swapaxes(-1, -2).reshape(w.shape)

    def column(b):
        return b.reshape(-1, P).T

    L0, L1 = "L0_xattn_", "L1_xattn_"
    wk0 = heads_inner(g[L0 + "Wk"], KV0, D0)
    bk0 = heads_inner(g[L0 + "bk"], KV0, D0)
    turned = lambda t: t.transpose(0, 2, 1).reshape(NB, C, P, P).transpose(0, 2, 1, 3)
    data = dict(
        x=g["x"], xT=turned(g["x"]), cT=turned(g["ctx_2048"]),
        mask=g["mask_Bx1xSxS2_ff0"].reshape(NB, P, P), kmask=g["mask_BxS2_bf1"],
        eye=np.eye(P, dtype=np.float32),
        cols=np.concatenate([
            column(heads_inner(g[L0 + "bq"], H0, D0)), column(np.concatenate([bk0, bk0])),
            column(heads_inner(g[L1 + "k_b"], H1, D1)), column(heads_inner(g[L1 + "q_b"], H1, D1)),
            column(g[L1 + "ln1_w"]), column(g[L1 + "ln1_b"]), column(g[L1 + "ln2_w"]), column(g[L1 + "ln2_b"]),
            column(g[L1 + "fc_b"])], axis=1),
        vecs=np.concatenate([g[L0 + "bv"], g[L1 + "v_b"], g[L0 + "bo"], g[L0 + "gamma"], g[L0 + "beta"],
                             g[L1 + "cproj_b"], g[L1 + "proj_b"]]),
        wqk=rows(np.concatenate([heads_inner(g[L0 + "Wq"], H0, D0), wk0, wk0], axis=1)),
        wv=rows(np.concatenate([g[L0 + "Wv"], g[L1 + "v_w"]], axis=1)), wo=rows(g[L0 + "Wo"]),
        wk1=rows(heads_inner(g[L1 + "k_w"], H1, D1)), wq1=rows(heads_inner(g[L1 + "q_w"], H1, D1)),
        wcp=rows(g[L1 + "cproj_w"]), wfc=rows(g[L1 + "fc_w"]), wpj=rows(g[L1 + "proj_w"]),
    )
    nc = bacc.Bacc("TRN2", target_bir_lowering=False, num_devices=1)
    arrays, args = {}, {}
    for name, a in data.items():
        a = np.ascontiguousarray(a)
        arrays["in_" + name] = a
        args[name] = nc.dram_tensor("in_" + name, a.shape, mb.dt.from_np(a.dtype), kind="ExternalInput").ap()
    args["out"] = nc.dram_tensor("out_0", _OUT, F32, kind="ExternalOutput").ap()
    build(nc, **args)
    r = run(nc, [arrays], core_ids=[0])
    return r.results[0]["out_0"]
```
